# Optimizing a Trainium2 kernel written in Bass

```python
import numpy as np
import jax
import jax.numpy as jnp

def _softmax(x, axis=-1):
    return jax.nn.softmax(x, axis=axis)

def _gelu(x):
    return jax.nn.gelu(x, approximate=True)

def _silu(x):
    return jax.nn.silu(x)

def _sigmoid(x):
    return jax.nn.sigmoid(x)

def _layernorm(x, axis=-1, eps=1e-05):
    m = jnp.mean(x, axis=axis, keepdims=True)
    v = jnp.var(x, axis=axis, keepdims=True)
    return (x - m) / jnp.sqrt(v + eps)

def _scatter_add(tgt, idx, src, axis=0):
    return tgt.at[idx].add(src)

def _segment_sum(src, seg, n):
    return jax.ops.segment_sum(src, seg, n)
kernel_name = 'mk_seq_preln_d1_jaxref_r8_1acb8f'

def setup_inputs(seed: int=0):
    np.random.seed(seed)
    _w = jnp.asarray

    def _L0_attn_setup():
        import math
        import jax, jax.numpy as jnp
        import numpy as np
        NUM_HEADS = 32
        HIDDEN = 512
        HEAD_DIM = HIDDEN // NUM_HEADS
        NEG_INF = -1e+30

        def _alibi_slopes(n: int) -> jnp.ndarray:
            cp2 = 2 ** math.floor(math.log2(n))
            base = 2.0 ** (-2.0 ** (-(math.log2(cp2) - 3)))
            slopes = base ** np.arange(1, cp2 + 1, dtype=np.float64)
            if cp2 != n:
                extra_base = 2.0 ** (-2.0 ** (-(math.log2(2 * cp2) - 3)))
                rem = min(cp2, n - cp2)
                extra = extra_base ** np.arange(1, 1 + 2 * rem, 2, dtype=np.float64)
                slopes = np.concatenate([slopes, extra])
            return jnp.asarray(slopes, dtype=jnp.float32)
        key = jax.random.key(seed)
        k1, k2, k3 = jax.random.split(key, 3)
        B, S = (2, 256)
        hidden_states = jax.random.normal(k1, (B, S, HIDDEN), dtype=jnp.float32)
        Wqkv = jax.random.normal(k2, (HIDDEN, NUM_HEADS * HEAD_DIM + 2 * HEAD_DIM), dtype=jnp.float32) * 0.02
        Wo = jax.random.normal(k3, (HIDDEN, HIDDEN), dtype=jnp.float32) * 0.02
        return {'hidden_states': hidden_states, 'Wqkv': Wqkv, 'Wo': Wo}
    _L0_attn_in = _L0_attn_setup()

    def _L0_ffn_setup():
        import jax, jax.numpy as jnp
        import numpy as np
        BATCH, TOK, DIM, OUT = (4, 256, 512, 512)
        E, R, TOP_K = (8, 16, 2)
        SCALING = 16.0 / R
        key = jax.random.key(seed)
        ks = jax.random.split(key, 6)
        return {'x': jax.random.normal(ks[0], (BATCH, TOK, DIM), dtype=jnp.float32), 'W_base': jax.random.normal(ks[1], (OUT, DIM), dtype=jnp.float32) / np.sqrt(DIM), 'b_base': jax.random.normal(ks[2], (OUT,), dtype=jnp.float32) * 0.01, 'W_gate': jax.random.normal(ks[3], (E, DIM), dtype=jnp.float32) * 0.01, 'A': jax.random.normal(ks[4], (E, R, DIM), dtype=jnp.float32) / np.sqrt(DIM), 'B': jax.random.normal(ks[5], (OUT, OUT // OUT * R * 0 + R), dtype=jnp.float32)[None].repeat(E, 0) * 0.0 + jax.random.normal(ks[5], (E, OUT, R), dtype=jnp.float32) * 0.02}
    _L0_ffn_in = _L0_ffn_setup()
    _d = {'L0_attn_hidden_states': _L0_attn_in['hidden_states'], 'L0_attn_Wqkv': _L0_attn_in['Wqkv'], 'L0_attn_Wo': _L0_attn_in['Wo'], 'L0_ffn_W_base': _L0_ffn_in['W_base'], 'L0_ffn_b_base': _L0_ffn_in['b_base'], 'L0_ffn_W_gate': _L0_ffn_in['W_gate'], 'L0_ffn_A': _L0_ffn_in['A'], 'L0_ffn_B': _L0_ffn_in['B']}
    _x0 = _d['L0_attn_hidden_states']
    _d['L0_attn_hidden_states'] = jax.random.normal(jax.random.fold_in(jax.random.key(seed), 1), (2, 1024, 512), dtype=_x0.dtype)
    del _x0
    return _d

def reference(L0_attn_hidden_states, L0_attn_Wqkv, L0_attn_Wo, L0_ffn_W_base, L0_ffn_b_base, L0_ffn_W_gate, L0_ffn_A, L0_ffn_B):

    def _L0_attn_ref(hidden_states, Wqkv, Wo):
        import math
        import jax, jax.numpy as jnp
        import numpy as np
        NUM_HEADS = 32
        HIDDEN = 512
        HEAD_DIM = HIDDEN // NUM_HEADS
        NEG_INF = -1e+30

        def _alibi_slopes(n: int) -> jnp.ndarray:
            cp2 = 2 ** math.floor(math.log2(n))
            base = 2.0 ** (-2.0 ** (-(math.log2(cp2) - 3)))
            slopes = base ** np.arange(1, cp2 + 1, dtype=np.float64)
            if cp2 != n:
                extra_base = 2.0 ** (-2.0 ** (-(math.log2(2 * cp2) - 3)))
                rem = min(cp2, n - cp2)
                extra = extra_base ** np.arange(1, 1 + 2 * rem, 2, dtype=np.float64)
                slopes = np.concatenate([slopes, extra])
            return jnp.asarray(slopes, dtype=jnp.float32)
        B, S, H = hidden_states.shape
        nH, d = (NUM_HEADS, HEAD_DIM)
        scale = d ** (-0.5)
        qkv = hidden_states @ Wqkv
        q = qkv[..., :nH * d].reshape(B, S, nH, d)
        k = qkv[..., nH * d:nH * d + d]
        v = qkv[..., nH * d + d:]
        scores = jnp.einsum('bqhd,bkd->bhqk', q, k) * scale
        pos_q = jnp.arange(S)[:, None]
        pos_k = jnp.arange(S)[None, :]
        slopes = _alibi_slopes(nH)
        alibi = slopes[:, None, None] * (pos_k - pos_q).astype(jnp.float32)
        causal = pos_k <= pos_q
        scores = jnp.where(causal[None, None], scores + alibi[None], NEG_INF)
        probs = jax.nn.softmax(scores, axis=-1)
        attn = jnp.einsum('bhqk,bkd->bqhd', probs, v).reshape(B, S, H)
        return attn @ Wo

    def _L0_ffn_ref(x, W_base, b_base, W_gate, A, B):
        import jax, jax.numpy as jnp
        import numpy as np
        BATCH, TOK, DIM, OUT = (4, 256, 512, 512)
        E, R, TOP_K = (8, 16, 2)
        SCALING = 16.0 / R
        result = jnp.einsum('bnd,od->bno', x, W_base) + b_base
        logits = jnp.einsum('bnd,ed->bne', x, W_gate)
        probs = jax.nn.softmax(logits.astype(jnp.float32), axis=-1)
        top_p, top_i = jax.lax.top_k(probs, TOP_K)
        top_p = top_p / jnp.sum(top_p, axis=-1, keepdims=True)
        top_p = top_p.astype(x.dtype)
        route_w = jnp.sum(jax.nn.one_hot(top_i, E, dtype=x.dtype) * top_p[..., None], axis=-2)
        h = jnp.einsum('bnd,erd->bner', x, A)
        hw = h * route_w[..., None]
        delta = jnp.einsum('bner,eor->bno', hw, B)
        return result + delta * SCALING
    x = L0_attn_hidden_states
    x = x + _L0_attn_ref(_layernorm(x, axis=-1), L0_attn_Wqkv, L0_attn_Wo)
    x = x + _L0_ffn_ref(_layernorm(x, axis=-1), L0_ffn_W_base, L0_ffn_b_base, L0_ffn_W_gate, L0_ffn_A, L0_ffn_B)
    return x

_drawn_inputs = setup_inputs


def setup_inputs(seed=0):
    import zlib

    import numpy as np

    out = dict(_drawn_inputs(seed))
    spreads = {}
    factors = {'L0_ffn_b_base': 8.0}
    for name, (base, spread) in spreads.items():
        noise = np.random.default_rng([zlib.crc32(name.encode()), seed]).standard_normal(out[name].shape)
        drawn = base * np.exp(spread * noise) if base else spread * noise
        out[name] = jnp.asarray(drawn.astype(out[name].dtype))
    for name, factor in factors.items():
        out[name] = (out[name] * factor).astype(out[name].dtype)
    return out
```

```python
from contextlib import ExitStack

import concourse.bass as bass
from concourse import mybir

F32 = mybir.dt.float32
BF16 = mybir.dt.bfloat16
U32 = mybir.dt.uint32
ALU = mybir.AluOpType
ACT = mybir.ActivationFunctionType
AX_X = mybir.AxisListType.X

P = 128
B, S, D = 2, 1024, 512
H, DH = 32, 16
E, R = 8, 16
KC = D // P
CH = 512
QT = CH // P
NCH = B * S // CH
UH = 4
UP = H // UH
NU = NCH * UP
PAIRS = UP // 2
PARTS = ((0, 0), (0, 1), (0, 2), (1, 0), (1, 1), (2, 0))
ROW_ALIBI = len(PARTS) * DH
N_ALIBI = 10
ROW_MAX = ROW_ALIBI + N_ALIBI
ROWS = ROW_MAX + 3
N_STAIR = P // DH - 1
STAIR_ROWS = ROWS + N_STAIR
QSCALE = DH ** -0.5
EPS = 1e-5
VW = 32
TR_AT = 3
XW = E * R + E
NT = B * S // P
LINKS_PER_TILE = 16


class Chain:

    def __init__(self, eng, sem):
        self.eng, self.sem, self.n, self.i, self.per = eng, sem, 0, None, 0

    def link(self, ins, plain_next=False):
        ins.then_inc(self.sem, 1)
        self.n += 1
        self.eng.wait_ge(self.sem, self.n if self.i is None else self.n + self.i * self.per)
        if plain_next:
            self.eng.nop(nofuse=True)

    def enter(self, i, per):
        self.i, self.per, self.first = i, per, self.n

    def leave(self, times):
        assert self.n - self.first == self.per
        self.n, self.i = self.first + times * self.per, None


def is_late(u):
    return (u // UP) % 2


def key_tiles(u):
    return QT * (1 + is_late(u))


def max_slots(u):
    out = []
    for t in range(QT):
        if is_late(u):
            out += [("full", t, (j,)) for j in range(UH)]
        per = {1: 4, 2: 2, 3: 1, 4: 1}[t + 1]
        out += [("diag", t, tuple(range(j, j + per))) for j in range(0, UH, per)]
    return out


def step_slots(n):
    slots = max_slots(n) if n < NU else []
    if 1 <= n <= NU:
        slots = slots[:TR_AT] + [("turn", None, None)] + slots[TR_AT:]
    return slots


SLOT0 = [0]
for _n in range(NU + 3):
    SLOT0.append(SLOT0[-1] + len(step_slots(_n)))
TILE0 = [0]
for _u in range(NU):
    TILE0.append(TILE0[-1] + key_tiles(_u))
LATE0 = [0]
for _u in range(NU):
    LATE0.append(LATE0[-1] + is_late(_u))


def build(nc, x, wqkv, wo, wb, ag, lora, bias, ident_in, identb_in, mneg_in, kmask_in, kalibi_in, qalibi_in, stair_in, iota_in, out):
    with ExitStack() as ctx:
        def sb(name, shape, dt=F32):
            return ctx.enter_context(nc.sbuf_tensor(name, shape, dt))

        def sem(name):
            return ctx.enter_context(nc.semaphore(name))

        q_dram = nc.dram_tensor("q_dram", (B, 3, D, S), BF16, kind="Internal").ap()
        m_dram = nc.dram_tensor("m_dram", (NU, UH * QT, 3, P), BF16, kind="Internal").ap()
        o_dram = nc.dram_tensor("o_dram", (NU, P, CH), F32, kind="Internal").ap()
        sum_dram = nc.dram_tensor("sum_dram", (NU, UH, CH), F32, kind="Internal").ap()
        rcp_dram = nc.dram_tensor("rcp_dram", (NU, UH, CH), F32, kind="Internal").ap()

        AR = PAIRS * CH
        arena = sb("arena", [P, 2 * AR * 2 + H * CH])
        q_op = arena[:, 4 * AR:4 * AR + H * CH].bitcast(BF16).rearrange("p (c n) -> p c n", c=2)

        def heads_of(c):
            return arena[:, c * 2 * AR:c * 2 * AR + AR].rearrange("p (g q) -> p g q", g=PAIRS)

        def rcps_of(c):
            return arena[:, c * 2 * AR + AR:(c + 1) * 2 * AR].rearrange("p (g q) -> p g q", g=PAIRS)

        work = sb("work", [P, 4 * UH * CH])
        probs = work[:, :].rearrange("p (r j q) -> p r j q", r=4, j=UH)
        xnT = work[:, 0:2 * KC * CH].rearrange("p (r k q) -> p r k q", r=2, k=KC)
        q4 = work[:, 4096:4096 + 2 * CH].rearrange("p (r q) -> p r q", r=2)
        qpart = work[:, 5120:5120 + 6 * CH].bitcast(BF16).rearrange("p (r a q) -> p r a q", r=4, a=3)
        x2 = work[:, 0:NT * D].rearrange("p (n d) -> p n d", d=D)
        x_sb = sb("x_sb", [P, 2, QT, D])
        k_op = sb("k_op", [P, B, S], BF16)
        v_op = sb("v_op", [P, B * S // P, 2, VW])
        wqkv_sb = sb("wqkv_sb", [P, KC, D + 112])
        wo_sb = sb("wo_sb", [P, KC, D])
        wb_sb = sb("wb_sb", [P, KC, D])
        ag_sb = sb("ag_sb", [P, KC, XW])
        lora_sb = sb("lora_sb", [P, D])
        bias_sb = sb("bias_sb", [P, D])
        ident = sb("ident", [P, P])
        identb = sb("identb", [P, P], BF16)
        mneg = sb("mneg", [P, P], BF16)
        kmask = sb("kmask", [P, 3])
        iota = sb("iota", [P, E])
        kv = sb("kv", [112, CH])
        k_rest = sb("k_rest", [96, CH])
        k_part = sb("k_part", [96, 3, CH], BF16)
        k_sum = sb("k_sum", [96, CH])
        stats = sb("stats", [P, QT, 6])
        mv = sb("mv", [P, QT, 2])
        ve = sb("ve", [P, QT])
        lnv = sb("lnv", [P, QT])
        rstd = sb("rstd", [P, QT])
        newt = sb("newt", [P, QT])
        negm = sb("negm", [P, 2, 2, UH * QT])
        m_t = sb("m_t", [UH * QT, 2, P])
        m_rest = sb("m_rest", [UH * QT, P])
        m_part = sb("m_part", [UH * QT, 2, 3, P], BF16)
        o_sb = sb("o_sb", [P, 2, CH])
        sums = sb("sums", [P, P])
        x1, x1b, xn2 = x_sb[:, 0, 0:2], x_sb[:, 0, 2:4], x_sb[:, 1, 0:2]
        xn2T = x_sb[:, 1, 2:4].rearrange("p r (k q) -> p r k q", k=KC)
        old_w = wqkv_sb[:, :, :].rearrange("p k n -> p (k n)")
        att = old_w[:, 0:2 * D].rearrange("p (r g q) -> p r g q", r=2, g=PAIRS)
        y_sb = old_w[:, 2 * D:4 * D].rearrange("p (r d) -> p r d", r=2)
        ff = sb("ff", [P, 2, 64])
        idx8 = sb("idx8", [P, 2, 8], U32)
        hw = sb("hw", [P, 2, E * R])
        hwT = sb("hwT", [P, 2, P])

        psum = ctx.enter_context(nc.psum_tensor("psum", [P, 8, 512], F32))

        w_in = sem("w_in")
        w2_in = sem("w2_in")
        ones_set = sem("ones_set")
        x_in = [sem("x_in0"), sem("x_in1")]
        var_ready = sem("var_ready")
        ln_done = sem("ln_done")
        rstd_guess = sem("rstd_guess")
        xn_ready = sem("xn_ready")
        turned = sem("turned")
        xnT_ready = sem("xnT_ready")
        proj_full = sem("proj_full")
        proj_free = sem("proj_free")
        q_hi_ready = sem("q_hi_ready")
        q_split = sem("q_split")
        q_stored = sem("q_stored")
        vt_full = sem("vt_full")
        v_ready = sem("v_ready")
        k_ready = sem("k_ready")
        dve_chain = sem("dve_chain")
        q_loaded = sem("q_loaded")
        slot_full = sem("slot_full")
        slot_free = sem("slot_free")
        max_late = sem("max_late")
        pool_chain = sem("pool_chain")
        m_split = sem("m_split")
        m_stored = sem("m_stored")
        m_loaded = sem("m_loaded")
        s_full = sem("s_full")
        exp_done = sem("exp_done")
        diag_done = sem("diag_done")
        pv_done = sem("pv_done")
        o_copied = sem("o_copied")
        o_stored = sem("o_stored")
        sums_in = sem("sums_in")
        rcp_ready = sem("rcp_ready")
        rcp_stored = sem("rcp_stored")
        heads_in = [sem(f"heads_in{c}") for c in range(NCH)]
        x2_in = [sem(f"x2_in{c}") for c in range(NCH)]
        att_ready = sem("att_ready")
        y_full = sem("y_full")
        x1_ready = sem("x1_ready")
        var2_ready = sem("var2_ready")
        ln2_done = sem("ln2_done")
        guess2 = sem("guess2")
        xn2_ready = sem("xn2_ready")
        x1b_ready = sem("x1b_ready")
        turned2 = sem("turned2")
        xn2T_ready = sem("xn2T_ready")
        h_full = sem("h_full")
        gap_ready = sem("gap_ready")
        e2_ready = sem("e2_ready")
        hw_ready = sem("hw_ready")
        hw_turned = sem("hw_turned")
        hwT_ready = sem("hwT_ready")
        z_full = sem("z_full")
        y_ready = sem("y_ready")
        out_sem = [sem("out_sem0"), sem("out_sem1")]

        block = ctx.enter_context(nc.Block())
        x_rows = x.rearrange("(c t p) d -> c p t d", t=QT, p=P)
        out_rows = out.rearrange("(n p) d -> n p d", p=P)
        N_W, N_W2 = 10, 5

        def at_loop(base, i, per):
            return base if i is None else base + i * per

        @block.sync
        def _(sp):
            sp.dma_start(x_sb[:, 0], x_rows[0]).then_inc(x_in[0], 16)
            sp.dma_start(ident[:], ident_in).then_inc(w_in, 16)
            sp.dma_start(wqkv_sb[:], wqkv.rearrange("(k p) n -> p k n", p=P)).then_inc(w_in, 16)
            sp.dma_start(x_sb[:, 1], x_rows[1]).then_inc(x_in[1], 16)
            sp.dma_start(identb[:], identb_in).then_inc(w_in, 16)
            sp.dma_start(mneg[:], mneg_in).then_inc(w_in, 16)
            sp.dma_start(kmask[:], kmask_in).then_inc(w_in, 16)
            for b in range(B):
                sp.dma_start(k_op[ROW_ALIBI:STAIR_ROWS, b, :], kalibi_in).then_inc(w_in, 16)
            for a in range(2):
                sp.dma_start(q_op[ROWS:STAIR_ROWS, a, :], stair_in).then_inc(w_in, 16)
            sp.dma_start(iota[:], iota_in).then_inc(w_in, 16)
            for c in (2, 3):
                sp.wait_ge(turned, QT * (c - 1))
                sp.dma_start(x_sb[:, c % 2], x_rows[c]).then_inc(x_in[c % 2], 16)
            sp.dma_start(wo_sb[:], wo.rearrange("(k p) n -> p k n", p=P)).then_inc(w2_in, 16)
            sp.dma_start(wb_sb[:], wb.rearrange("(k p) n -> p k n", p=P)).then_inc(w2_in, 16)
            sp.dma_start(ag_sb[:], ag.rearrange("(k p) n -> p k n", p=P)).then_inc(w2_in, 16)
            sp.dma_start(lora_sb[:], lora).then_inc(w2_in, 16)
            sp.dma_start(bias_sb[:], bias).then_inc(w2_in, 16)

            def load_queries(c):
                b, late = c // 2, c % 2
                sp.wait_ge(q_loaded, 16 * 7 * c)
                sp.wait_ge(q_stored, 16 * 4 * (c + 1))
                for n, (a, _) in enumerate(PARTS):
                    sp.dma_start(q_op[DH * n:DH * (n + 1), c % 2, :].rearrange("p (h q) -> p h q", h=H),
                                 q_dram[b, a, :, late * CH:(late + 1) * CH].rearrange("(h d) q -> d h q", d=DH)
                                 ).then_inc(q_loaded, 16)
                sp.dma_start(q_op[ROW_ALIBI:ROW_MAX, c % 2, :].rearrange("p (h q) -> p h q", h=H),
                             qalibi_in[:, :, late * CH:(late + 1) * CH]).then_inc(q_loaded, 16)

            def plain_next():
                sp.nop(nofuse=True)

            def store_unit(u, i=None):
                uu = at_loop(u, i, 2)
                sp.wait_ge(o_copied, at_loop(u + 1, i, 2))
                plain_next()
                sp.wait_ge(o_stored, at_loop(32 * u, i, 64))
                plain_next()
                sp.dma_start(o_dram[bass.ds(uu, 1)].rearrange("u p q -> (u p) q"), o_sb[:, u % 2]).then_inc(o_stored, 16)
                ones = DH * (1 - u % 2)
                sp.dma_start(sum_dram[bass.ds(uu, 1)].rearrange("u j q -> (u j) q"),
                             o_sb[ones:P:VW, u % 2]).then_inc(o_stored, 16)

            def max_rows(u, i=None):
                uu = at_loop(u, i, 2)
                sp.wait_ge(m_split, at_loop(u + 1, i, 2))
                plain_next()
                sp.dma_start(m_dram[bass.ds(uu, 1)].rearrange("u n a q -> (u n) a q"), m_part[:, u % 2]).then_inc(m_stored, 16)
                sp.wait_ge(m_stored, at_loop(16 * (u + 1), i, 32))
                plain_next()
                g = (u % UP) // 2
                first = at_loop(8 * g + u % 2, i, 8) * CH
                c = u // UP
                if u:
                    sp.wait_ge(m_loaded, at_loop(64 * u, i, 128))
                    plain_next()
                for j in range(UH):
                    sp.dma_start(q_op[ROW_MAX:ROWS, c % 2, bass.ds(first + 2 * j * CH, CH)].rearrange("p (t q) -> p t q", t=QT),
                                 m_dram[bass.ds(uu, 1), QT * j:QT * (j + 1)].rearrange("u t a q -> a (u t) q")
                                 ).then_inc(m_loaded, 16)

            def load_sums(c):
                sp.wait_ge(o_stored, 32 * UP * (c + 1))
                if c:
                    sp.wait_ge(rcp_stored, 16 * c)
                sp.dma_start(sums[:], sum_dram[UP * c:UP * (c + 1)].rearrange("u j (s q) -> (u j s) q", s=QT)
                             ).then_inc(sums_in, 16)

            def store_rcps(c):
                sp.wait_ge(rcp_ready, c + 1)
                sp.dma_start(rcp_dram[UP * c:UP * (c + 1)].rearrange("u j (s q) -> (u j s) q", s=QT), sums[:]
                             ).then_inc(rcp_stored, 16)

            def load_heads(c):
                sp.wait_ge(o_stored, 32 * UP * (c + 1))
                sp.wait_ge(rcp_stored, 16 * (c + 1))
                o_c = o_dram[UP * c:UP * (c + 1)].rearrange("(g s) p q -> s p g q", s=2)
                r_c = rcp_dram[UP * c:UP * (c + 1)].rearrange("(g s) j q -> s j g q", s=2)
                for j in range(UH):
                    for s in range(2):
                        p0 = VW * j + DH * s
                        sp.dma_start(heads_of(c)[p0:p0 + DH], o_c[s, p0:p0 + DH]).then_inc(heads_in[c], 16)
                        sp.dma_start(rcps_of(c)[p0:p0 + DH],
                                     r_c[s, j:j + 1].broadcast_to((DH, PAIRS, CH))).then_inc(heads_in[c], 16)

            load_queries(0)
            for c in range(NCH):
                u0 = UP * c
                for u in (u0, u0 + 1):
                    max_rows(u)
                    if u >= 2:
                        store_unit(u - 2)
                if c + 1 < NCH:
                    if c:
                        sp.wait_ge(s_full, 2 * TILE0[u0])
                    load_queries(c + 1)
                if c >= 2:
                    store_rcps(c - 2)
                if c == 0:
                    for s in range(2):
                        max_rows(2 + s)
                        store_unit(s)
                with sp.Fori(1 if c == 0 else 0, PAIRS - 1) as i:
                    for s in range(2):
                        max_rows(u0 + 2 + s, i)
                        store_unit(u0 + s, i)
                if c >= 1:
                    load_sums(c - 1)
            load_heads(0)
            store_unit(NU - 2)
            store_unit(NU - 1)
            sp.wait_ge(pv_done, TILE0[NU])
            sp.dma_start(x2[:, 0:QT], x_rows[0]).then_inc(x2_in[0], 16)
            store_rcps(2)
            load_sums(3)
            load_heads(1)
            sp.dma_start(x2[:, QT:2 * QT], x_rows[1]).then_inc(x2_in[1], 16)
            store_rcps(3)
            for c in (2, 3):
                load_heads(c)
                sp.dma_start(x2[:, QT * c:QT * (c + 1)], x_rows[c]).then_inc(x2_in[c], 16)
            with sp.Fori(0, NT // 2) as i:
                for s in range(2):
                    sp.wait_ge(y_ready, i * 2 + s + 1)
                    plain_next()
                    sp.dma_start(out_rows[bass.ds(i * 2 + s, 1)].rearrange("n p d -> (n p) d"), y_sb[:, s]).then_inc(out_sem[s], 16)
            for s in range(2):
                sp.wait_ge(out_sem[s], 16 * (NT // 2))

        @block.tensor
        def _(pe):
            pe.wait_ge(w_in, 16 * N_W)

            def transposes(c):
                for t in range(QT):
                    n = QT * c + t
                    pe.wait_ge(xn_ready, n + 1)
                    if n >= 2:
                        pe.wait_ge(xnT_ready, n - 1)
                    for k in range(KC):
                        last = nc.tensor.transpose(psum[:, n % 2, k * P:(k + 1) * P],
                                                   x_sb[:, c % 2, t, k * P:(k + 1) * P], ident[:])
                    last.then_inc(turned, 1)

            def project(c, m):
                if m == 0:
                    pe.wait_ge(xnT_ready, QT * (c + 1))
                if c:
                    pe.wait_ge(proj_free, 5 * (c - 1) + m + 1)
                width = P if m < 4 else 112
                for k in range(KC):
                    last = nc.tensor.matmul(psum[0:width, 2 + m, :], wqkv_sb[:, k, P * m:P * m + width], xnT[:, c % 2, k, :],
                                            start=(k == 0), stop=(k == KC - 1))
                last.then_inc(proj_full, 1)

            def values(c):
                pe.wait_ge(proj_free, 5 * c + 5)
                if c:
                    pe.wait_ge(v_ready, c)
                for t in range(QT):
                    last = nc.tensor.transpose(psum[:, 7, 112 * t:112 * (t + 1)], kv[:, t * P:(t + 1) * P], ident[0:112, 0:112])
                last.then_inc(vt_full, 1)

            transposes(0)
            for c in range(NCH):
                for m in range(5):
                    project(c, m)
                    if m == 0 and c:
                        values(c - 1)
                    if m == 2 and c + 1 < NCH:
                        transposes(c + 1)
            values(NCH - 1)

            def max_slot(n, x_, r, i):
                kind, t, js = x_
                idx = SLOT0[n] + r
                per = 2 * len(step_slots(n)) if i is not None else 0
                if idx >= 2:
                    pe.wait_ge(slot_free, at_loop(idx - 1, i, per))
                bank = psum[:, idx % 2]
                if kind == "turn":
                    u = n - 1
                    if is_late(u):
                        pe.wait_ge(max_late, at_loop(LATE0[u] + 1, i, 2))
                    else:
                        pe.wait_ge(slot_free, at_loop(SLOT0[n], i, per))
                    nc.tensor.transpose(bank[0:UH * QT, 0:P], negm[:, u % 2, 0, :], ident[:]).then_inc(slot_full, 1)
                    return
                c = n // UP
                b, late = c // 2, c % 2
                width = P * (t + 1) if kind == "diag" else CH
                k0 = CH * late if kind == "diag" else 0
                g = (n % UP) // 2
                for a, j in enumerate(js):
                    col = at_loop(8 * g + 2 * j + n % 2, i, 8) * CH + t * P
                    last = nc.tensor.matmul(bank[:, a * width:(a + 1) * width], q_op[0:ROW_MAX, c % 2, bass.ds(col, P)],
                                            k_op[0:ROW_MAX, b, k0:k0 + width],
                                            start=(a == 0), stop=(kind == "full"), skip_group_check=True)
                if kind == "diag":
                    w = len(js) * width
                    masked = bank[:, 0:w].rearrange("p (a k) -> p a k", a=len(js))[:, :, width - P:width]
                    last = nc.tensor.matmul(masked, identb[:], mneg[:, None, :].broadcast_to((P, len(js), P)),
                                            start=False, stop=True, skip_group_check=True)
                last.then_inc(slot_full, 1)

            def scores(u, t, i):
                c = u // UP
                b, late = c // 2, c % 2
                off = max(0, P * (t - QT * late))
                g = (u % UP) // 2
                tiles = key_tiles(u)
                if t == 0:
                    pe.wait_ge(m_loaded, at_loop(64 * (u + 1), i, 128))
                for hp in range(2):
                    idx = 2 * (TILE0[u] + t) + hp
                    if idx >= 2:
                        pe.wait_ge(exp_done, at_loop(idx - 1, i, 4 * tiles))
                    for a in range(2):
                        col = at_loop(8 * g + 2 * (2 * hp + a) + u % 2, i, 8) * CH + off
                        bank = psum[:, 2 + 2 * (idx % 2) + a]
                        diag = P if t >= QT * late else 0
                        if diag:
                            last = nc.tensor.matmul(bank[:, 0:P], k_op[0:STAIR_ROWS, b, t * P:(t + 1) * P],
                                                    q_op[0:STAIR_ROWS, c % 2, bass.ds(col, P)], start=True, stop=True)
                        if off + diag < CH:
                            last = nc.tensor.matmul(bank[:, diag:CH - off], k_op[0:ROWS, b, t * P:(t + 1) * P],
                                                    q_op[0:ROWS, c % 2, bass.ds(col + diag, CH - off - diag)],
                                                    start=True, stop=True)
                    last.then_inc(s_full, 1)

            def values_product(u, t, i):
                c = u // UP
                b, late = c // 2, c % 2
                off = max(0, P * (t - QT * late))
                tiles = key_tiles(u)
                n = TILE0[u] + t
                if t == 0 and u >= 2:
                    pe.wait_ge(o_copied, at_loop(u - 1, i, 2))
                pe.wait_ge(exp_done, at_loop(2 * n + 2, i, 4 * tiles))
                if t >= QT * late:
                    pe.wait_ge(diag_done, at_loop(QT * u + t - QT * late + 1, i, 2 * QT))
                for j in range(UH):
                    last = nc.tensor.matmul(psum[VW * j:VW * (j + 1), 6 + u % 2, off:CH], v_op[:, b * (S // P) + t, u % 2, :],
                                            probs[:, t % 4, j, 0:CH - off], start=(t == 0), stop=(t == tiles - 1))
                last.then_inc(pv_done, 1)

            def step(n, i=None):
                slots = [(lambda r=r, x_=x_: max_slot(n, x_, r, i)) for r, x_ in enumerate(step_slots(n))]
                pieces = []
                u = n - 2
                if 0 <= u < NU:
                    tiles = key_tiles(u)
                    for t in range(tiles + 1):
                        if t < tiles:
                            pieces.append(lambda t=t: scores(u, t, i))
                        if t:
                            pieces.append(lambda t=t: values_product(u, t - 1, i))
                done = 0
                for k, piece in enumerate(pieces):
                    upto = -(-len(slots) * (k + 1) // max(1, len(pieces)))
                    for f in slots[done:upto]:
                        f()
                    done = max(done, upto)
                    piece()
                for f in slots[done:]:
                    f()

            pe.wait_ge(v_ready, NCH)
            pe.wait_ge(k_ready, NCH)
            for c in range(NCH):
                pe.wait_ge(q_loaded, 16 * 7 * (c + 1))
                step(UP * c)
                step(UP * c + 1)
                with pe.Fori(0, PAIRS - 1) as i:
                    for s in range(2):
                        step(UP * c + 2 + s, i)
            step(NU)
            step(NU + 1)

            pe.wait_ge(w2_in, 16 * N_W2)

            def out_proj(n, i):
                pe.wait_ge(att_ready, at_loop(n + 1, i, 2))
                if n >= 2:
                    pe.wait_ge(x1_ready, at_loop(n - 1, i, 2))
                for g in range(PAIRS):
                    last = nc.tensor.matmul(psum[:, n % 2], att[:, n % 2, g, :], wo_sb[:, g, :], start=(g == 0), stop=(g == PAIRS - 1))
                last.then_inc(y_full, 1)

            def turn_xn2(n, i):
                pe.wait_ge(xn2_ready, at_loop(n + 1, i, 2))
                if n >= 2:
                    pe.wait_ge(xn2T_ready, at_loop(n - 1, i, 2))
                for k in range(KC):
                    last = nc.tensor.transpose(psum[:, 2 + n % 2, k * P:(k + 1) * P], xn2[:, n % 2, k * P:(k + 1) * P], ident[:])
                last.then_inc(turned2, 1)

            def base_and_lora_in(n, i):
                pe.wait_ge(xn2T_ready, at_loop(n + 1, i, 2))
                if n >= 1:
                    pe.wait_ge(hw_ready, at_loop(n, i, 2))
                for k in range(KC):
                    last = nc.tensor.matmul(psum[:, 4, 0:XW], xn2T[:, n % 2, k, :], ag_sb[:, k, :], start=(k == 0), stop=(k == KC - 1))
                last.then_inc(h_full, 1)
                if n >= 2:
                    pe.wait_ge(y_ready, at_loop(n - 1, i, 2))
                for k in range(KC):
                    nc.tensor.matmul(psum[:, 6 + n % 2], xn2T[:, n % 2, k, :], wb_sb[:, k, :], start=(k == 0), stop=False)

            def turn_hw(n, i):
                pe.wait_ge(hw_ready, at_loop(n + 1, i, 2))
                if n >= 1:
                    pe.wait_ge(hwT_ready, at_loop(n, i, 2))
                nc.tensor.transpose(psum[:, 5, 0:P], hw[:, n % 2], ident[:]).then_inc(hw_turned, 1)

            def lora_out(n, i):
                pe.wait_ge(hwT_ready, at_loop(n + 1, i, 2))
                nc.tensor.matmul(psum[:, 6 + n % 2], hwT[:, n % 2], lora_sb[:], start=False, stop=True).then_inc(z_full, 1)

            def ffn_step(n, i=None):
                if n < NT:
                    out_proj(n, i)
                if 1 <= n <= NT:
                    turn_xn2(n - 1, i)
                if 2 <= n:
                    turn_hw(n - 2, i)
                if 1 <= n <= NT:
                    base_and_lora_in(n - 1, i)
                if 2 <= n:
                    lora_out(n - 2, i)

            for n in range(QT):
                ffn_step(n)
            for c in range(1, NCH):
                with pe.Fori(0, QT // 2) as i:
                    for s in range(2):
                        ffn_step(QT * c + s, i)
            ffn_step(NT)
            ffn_step(NT + 1)

        @block.scalar
        def _(act):
            def rstd_first(c):
                act.wait_ge(var_ready, c + 1)
                nc.scalar.activation(lnv[:], ve[:], ACT.Ln).then_inc(ln_done, 1)
                act.wait_ge(ln_done, c + 1)
                nc.scalar.activation(rstd[:], lnv[:], ACT.Exp, scale=-0.5).then_inc(rstd_guess, 1)

            def xnT_copies(c):
                for t in range(QT):
                    n = QT * c + t
                    act.wait_ge(turned, n + 1)
                    if t == 0 and c >= 2:
                        act.wait_ge(proj_full, 5 * (c - 1))
                    nc.scalar.copy(xnT[:, c % 2, :, t * P:(t + 1) * P],
                                   psum[:, n % 2].rearrange("p (k q) -> p k q", k=KC)).then_inc(xnT_ready, 1)

            def query_hi(c, m):
                n = 4 * c + m
                act.wait_ge(proj_full, 5 * c + m + 1)
                if n >= 2:
                    act.wait_ge(q_split, n - 1)
                if n >= 4:
                    act.wait_ge(q_stored, 16 * (n - 3))
                nc.scalar.mul(q4[:, n % 2], psum[:, 2 + m], QSCALE).then_inc(proj_free, 1)
                act.wait_ge(proj_free, 5 * c + m + 1)
                nc.scalar.copy(qpart[:, n % 4, 0], q4[:, n % 2]).then_inc(q_hi_ready, 1)

            def keys_values(c):
                act.wait_ge(proj_full, 5 * c + 5)
                if c:
                    act.wait_ge(k_ready, c)
                    act.wait_ge(vt_full, c)
                nc.scalar.copy(kv[:], psum[0:112, 6]).then_inc(proj_free, 1)

            act.preload_act_table_set("natural_log_exp_and_others")
            rstd_first(0)
            xnT_copies(0)
            rstd_first(1)
            for c in range(NCH):
                for m in range(4):
                    query_hi(c, m)
                    if m == 2 and c + 1 < NCH:
                        xnT_copies(c + 1)
                keys_values(c)
                if c + 2 < NCH:
                    rstd_first(c + 2)

            def exps(u, t, i):
                tiles = key_tiles(u)
                off = max(0, P * (t - QT * is_late(u)))
                n = TILE0[u] + t
                if n >= 4:
                    act.wait_ge(pv_done, at_loop(n - 3, i, 2 * tiles))
                for hp in range(2):
                    idx = 2 * n + hp
                    act.wait_ge(s_full, at_loop(idx + 1, i, 4 * tiles))
                    nc.scalar.activation(probs[:, t % 4, 2 * hp:2 * hp + 2, 0:CH - off],
                                         psum[:, 2 + 2 * (idx % 2):4 + 2 * (idx % 2), 0:CH - off], ACT.Exp).then_inc(exp_done, 1)

            def copy_unit(u, i, step_tiles):
                act.wait_ge(pv_done, at_loop(TILE0[u + 1], i, 2 * step_tiles))
                if u >= 2:
                    act.wait_ge(o_stored, at_loop(32 * (u - 1), i, 64))
                nc.scalar.copy(o_sb[:, u % 2], psum[:, 6 + u % 2]).then_inc(o_copied, 1)

            def unit(u, i=None):
                for t in range(key_tiles(u)):
                    exps(u, t, i)
                    if t == 1 and u:
                        copy_unit(u - 1, i, key_tiles(u))

            act.wait_ge(q_stored, 16 * 4 * NCH)
            for c in range(NCH):
                unit(UP * c)
                unit(UP * c + 1)
                with act.Fori(0, PAIRS - 1) as i:
                    unit(UP * c + 2, i)
                    unit(UP * c + 3, i)
            copy_unit(NU - 1, None, 0)

            def guess(n, i):
                act.wait_ge(var2_ready, at_loop(n + 1, i, 2))
                nc.scalar.activation(ff[:, n % 2, 2:3], ff[:, n % 2, 1:2], ACT.Ln).then_inc(ln2_done, 1)
                act.wait_ge(ln2_done, at_loop(n + 1, i, 2))
                nc.scalar.activation(ff[:, n % 2, 3:4], ff[:, n % 2, 2:3], ACT.Exp, scale=-0.5).then_inc(guess2, 1)

            def copy_xn2T(n, i):
                act.wait_ge(turned2, at_loop(n + 1, i, 2))
                if n >= 2:
                    act.wait_ge(z_full, at_loop(n - 1, i, 2))
                nc.scalar.copy(xn2T[:, n % 2], psum[:, 2 + n % 2].rearrange("p (k q) -> p k q", k=KC)).then_inc(xn2T_ready, 1)

            def second_weight(n, i):
                act.wait_ge(gap_ready, at_loop(n + 1, i, 2))
                nc.scalar.activation(ff[:, n % 2, 6:7], ff[:, n % 2, 5:6], ACT.Exp).then_inc(e2_ready, 1)

            def copy_hwT(n, i):
                act.wait_ge(hw_turned, at_loop(n + 1, i, 2))
                if n >= 2:
                    act.wait_ge(z_full, at_loop(n - 1, i, 2))
                nc.scalar.copy(hwT[:, n % 2], psum[:, 5, 0:P]).then_inc(hwT_ready, 1)

            def ffn_step(n, i=None):
                if 1 <= n <= NT:
                    copy_xn2T(n - 1, i)
                if 2 <= n:
                    copy_hwT(n - 2, i)
                if n < NT:
                    guess(n, i)
                if 1 <= n <= NT:
                    second_weight(n - 1, i)

            for n in range(QT):
                ffn_step(n)
            for c in range(1, NCH):
                with act.Fori(0, QT // 2) as i:
                    for s in range(2):
                        ffn_step(QT * c + s, i)
            ffn_step(NT)
            ffn_step(NT + 1)

        @block.vector
        def _(dve):
            chain = Chain(dve, dve_chain)
            link = chain.link

            nc.vector.memset(v_op[:], 1.0).then_inc(ones_set, 1)

            def newton(r, v, t):
                link(nc.vector.tensor_tensor(t, r, r, ALU.mult))
                link(nc.vector.tensor_tensor(t, t, v, ALU.mult))
                link(nc.vector.tensor_scalar(t, t, -0.5, 1.5, ALU.mult, ALU.add))
                link(nc.vector.tensor_tensor(r, r, t, ALU.mult))

            def norm(c):
                dve.wait_ge(x_in[c % 2], 16 * (c // 2 + 1))
                for t in range(QT):
                    last = nc.vector.bn_stats(stats[:, t], x_sb[:, c % 2, t])
                link(last)
                for t in range(QT):
                    last = nc.vector.bn_aggr(mv[:, t], stats[:, t])
                link(last)
                nc.vector.tensor_scalar(ve[:], mv[:, :, 1], EPS, None, ALU.add).then_inc(var_ready, 1)
                dve.wait_ge(rstd_guess, c + 1)
                dve.wait_ge(var_ready, c + 1)
                newton(rstd[:], ve[:], newt[:])
                for t in range(QT):
                    nc.vector.tensor_scalar(x_sb[:, c % 2, t], x_sb[:, c % 2, t], mv[:, t, 0:1], rstd[:, t:t + 1],
                                            ALU.subtract, ALU.mult).then_inc(xn_ready, 1)

            def split_queries(c):
                for m in range(4):
                    n = 4 * c + m
                    dve.wait_ge(q_hi_ready, n + 1)
                    link(nc.vector.tensor_tensor(q4[:, n % 2], q4[:, n % 2], qpart[:, n % 4, 0], ALU.subtract))
                    link(nc.vector.tensor_copy(qpart[:, n % 4, 1], q4[:, n % 2]))
                    nc.vector.tensor_tensor(qpart[:, n % 4, 2], q4[:, n % 2], qpart[:, n % 4, 1], ALU.subtract).then_inc(q_split, 1)

            def split_keys(c):
                dve.wait_ge(proj_free, 5 * c + 5)
                link(nc.vector.tensor_copy(k_part[:, 0], kv[0:96]))
                link(nc.vector.tensor_tensor(k_rest[:], kv[0:96], k_part[:, 0], ALU.subtract))
                link(nc.vector.tensor_copy(k_part[:, 1], k_rest[:]))
                link(nc.vector.tensor_tensor(k_part[:, 2], k_rest[:], k_part[:, 1], ALU.subtract))
                link(nc.vector.tensor_scalar(k_sum[:], k_part[:, 0], kmask[0:96, 0:1], None, ALU.mult))
                link(nc.vector.scalar_tensor_tensor(k_sum[:], k_part[:, 1], kmask[0:96, 1:2], k_sum[:], ALU.mult, ALU.add))
                nc.vector.scalar_tensor_tensor(k_op[0:96, c // 2, (c % 2) * CH:(c % 2 + 1) * CH], k_part[:, 2],
                                               kmask[0:96, 2:3], k_sum[:], ALU.mult, ALU.add).then_inc(k_ready, 1)

            def copy_values(c):
                dve.wait_ge(vt_full, c + 1)
                v = psum[:, 7, 0:QT * 112].rearrange("p (t n) -> p t n", t=QT)[:, :, 96:112]
                nc.vector.tensor_copy(v_op[:, QT * c:QT * (c + 1), 0, 0:DH], v)
                nc.vector.tensor_copy(v_op[:, QT * c:QT * (c + 1), 1, DH:VW], v).then_inc(v_ready, 1)

            dve.wait_ge(w_in, 16 * N_W)
            dve.wait_ge(ones_set, 1)
            norm(0)
            norm(1)
            for c in range(NCH):
                split_queries(c)
                split_keys(c)
                if c + 2 < NCH:
                    norm(c + 2)
                copy_values(c)

            def step(n, i=None):
                slots = step_slots(n)
                per = 2 * len(slots)
                for r, (kind, t, js) in enumerate(slots):
                    idx = SLOT0[n] + r
                    dve.wait_ge(slot_full, at_loop(idx + 1, i, per))
                    bank = psum[:, idx % 2]
                    if kind == "turn":
                        u = n - 1
                        if u >= 2:
                            dve.wait_ge(m_split, at_loop(u - 1, i, 2))
                        nc.vector.tensor_copy(m_t[:, u % 2], bank[0:UH * QT, 0:P]).then_inc(slot_free, 1)
                        continue
                    width = P * (t + 1) if kind == "diag" else CH
                    where = 1 if kind == "full" else 0
                    dst = negm[:, n % 2, where, :].rearrange("p (j t) -> p j t", t=QT)[:, js[0]:js[-1] + 1, t]
                    nc.vector.tensor_reduce(dst, bank[:, 0:len(js) * width].rearrange("p (a k) -> p a k", a=len(js)), AX_X, ALU.max,
                                            negate=True).then_inc(slot_free, 1)
                if n < NU and is_late(n):
                    dve.wait_ge(slot_free, at_loop(SLOT0[n + 1], i, per))
                    nc.vector.tensor_tensor(negm[:, n % 2, 0, :], negm[:, n % 2, 0, :], negm[:, n % 2, 1, :], ALU.min
                                            ).then_inc(max_late, 1)

            def reciprocals(c):
                dve.wait_ge(sums_in, 16 * (c + 1))
                nc.vector.reciprocal(sums[:], sums[:]).then_inc(rcp_ready, 1)

            for c in range(NCH):
                step(UP * c)
                step(UP * c + 1)
                if c >= 2:
                    reciprocals(c - 2)
                with dve.Fori(0, PAIRS - 1) as i:
                    for s in range(2):
                        step(UP * c + 2 + s, i)
            step(NU)
            reciprocals(2)

            def residual(n, i):
                dve.wait_ge(y_full, at_loop(n + 1, i, 2))
                if n >= 2:
                    dve.wait_ge(x1b_ready, at_loop(n - 1, i, 2))
                nc.vector.tensor_tensor(x1[:, n % 2], x2[:, bass.ds(at_loop(n, i, 2), 1)].rearrange("p n d -> p (n d)"), psum[:, n % 2], ALU.add).then_inc(x1_ready, 1)
                dve.wait_ge(x1_ready, at_loop(n + 1, i, 2))
                link(nc.vector.bn_stats(stats[:, n % 2], x1[:, n % 2]), plain_next=True)
                link(nc.vector.bn_aggr(mv[:, n % 2], stats[:, n % 2]))
                nc.vector.tensor_scalar(ff[:, n % 2, 1:2], mv[:, n % 2, 1:2], EPS, None, ALU.add).then_inc(var2_ready, 1)

            def norm2(n, i):
                dve.wait_ge(guess2, at_loop(n + 1, i, 2))
                newton(ff[:, n % 2, 3:4], ff[:, n % 2, 1:2], ff[:, n % 2, 4:5])
                if n >= 2:
                    dve.wait_ge(turned2, at_loop(n - 1, i, 2))
                nc.vector.tensor_scalar(xn2[:, n % 2], x1[:, n % 2], mv[:, n % 2, 0:1], ff[:, n % 2, 3:4],
                                        ALU.subtract, ALU.mult).then_inc(xn2_ready, 1)

            def route_first(n, i):
                f = ff[:, n % 2]
                dve.wait_ge(h_full, at_loop(n + 1, i, 2))
                link(nc.vector.tensor_copy(f[:, 8:16], psum[:, 4, E * R:XW]), plain_next=True)
                link(nc.vector.max(f[:, 16:24], f[:, 8:16]), plain_next=True)
                link(nc.vector.max_index(idx8[:, n % 2], f[:, 16:24], f[:, 8:16]))
                link(nc.vector.tensor_copy(f[:, 24:32], idx8[:, n % 2]))
                nc.vector.tensor_tensor(f[:, 5:6], f[:, 17:18], f[:, 16:17], ALU.subtract).then_inc(gap_ready, 1)

            def route_second(n, i):
                f = ff[:, n % 2]
                dve.wait_ge(e2_ready, at_loop(n + 1, i, 2))
                link(nc.vector.tensor_scalar(f[:, 7:8], f[:, 6:7], 1.0, None, ALU.add))
                link(nc.vector.reciprocal(f[:, 32:33], f[:, 7:8]))
                link(nc.vector.tensor_tensor(f[:, 33:34], f[:, 32:33], f[:, 6:7], ALU.mult))
                link(nc.vector.tensor_scalar(f[:, 40:48], iota[:], f[:, 24:25], f[:, 32:33], ALU.is_equal, ALU.mult))
                link(nc.vector.tensor_scalar(f[:, 48:56], iota[:], f[:, 25:26], f[:, 33:34], ALU.is_equal, ALU.mult))
                link(nc.vector.tensor_tensor(f[:, 56:64], f[:, 40:48], f[:, 48:56], ALU.add))
                if n >= 2:
                    dve.wait_ge(hw_turned, at_loop(n - 1, i, 2))
                nc.vector.tensor_tensor(hw[:, n % 2].rearrange("p (e r) -> p e r", e=E),
                                        psum[:, 4, 0:E * R].rearrange("p (e r) -> p e r", e=E),
                                        f[:, 56:64, None].broadcast_to((P, E, R)), ALU.mult).then_inc(hw_ready, 1)

            def finish(n, i):
                dve.wait_ge(z_full, at_loop(n + 1, i, 2))
                dve.wait_ge(x1b_ready, at_loop(n + 1, i, 2))
                if n >= 2:
                    dve.wait_ge(out_sem[n % 2], at_loop(16 * (n // 2), i, 16))
                nc.vector.tensor_tensor(y_sb[:, n % 2], x1b[:, n % 2], psum[:, 6 + n % 2], ALU.add).then_inc(y_ready, 1)

            def ffn_step(n, i=None):
                if n < NT:
                    residual(n, i)
                if 1 <= n <= NT:
                    route_first(n - 1, i)
                if n < NT:
                    norm2(n, i)
                if 1 <= n <= NT:
                    route_second(n - 1, i)
                if 2 <= n:
                    finish(n - 2, i)

            dve.wait_ge(x2_in[0], 16)
            ffn_step(0)
            ffn_step(1)
            reciprocals(3)
            ffn_step(2)
            ffn_step(3)
            for c in range(1, NCH):
                dve.wait_ge(x2_in[c], 16)
                with dve.Fori(0, QT // 2) as i:
                    chain.enter(i, 2 * LINKS_PER_TILE)
                    for s in range(2):
                        ffn_step(QT * c + s, i)
                    chain.leave(QT // 2)
            ffn_step(NT)
            ffn_step(NT + 1)

        @block.gpsimd
        def _(pool):
            for c in range(NCH):
                for m in range(4):
                    n = 4 * c + m
                    pool.wait_ge(q_split, n + 1)
                    if n:
                        pool.wait_ge(q_stored, 16 * n)
                    pool.dma_start(q_dram[c // 2, :, P * m:P * (m + 1), (c % 2) * CH:(c % 2 + 1) * CH].rearrange("a r q -> r a q"),
                                   qpart[:, n % 4]).then_inc(q_stored, 16)

            def plain_next():
                pool.nop(nofuse=True)

            def split_max(n, i):
                u = n - 1
                per = 2 * len(step_slots(n)) if i is not None else 0
                pool.wait_ge(slot_free, at_loop(SLOT0[n] + TR_AT * (n < NU) + 1, i, per))
                if u >= 2:
                    pool.wait_ge(m_stored, at_loop(16 * (u - 1), i, 32))
                plain_next()
                k = 4 * u
                mt, mp = m_t[:, u % 2], m_part[:, u % 2]
                nc.gpsimd.tensor_copy(mp[:, 0], mt).then_inc(pool_chain, 1)
                pool.wait_ge(pool_chain, at_loop(k + 1, i, 8))
                nc.gpsimd.tensor_tensor(out=m_rest[:], in0=mt, in1=mp[:, 0], op=ALU.subtract).then_inc(pool_chain, 1)
                pool.wait_ge(pool_chain, at_loop(k + 2, i, 8))
                plain_next()
                nc.gpsimd.tensor_copy(mp[:, 1], m_rest[:]).then_inc(pool_chain, 1)
                pool.wait_ge(pool_chain, at_loop(k + 3, i, 8))
                nc.gpsimd.tensor_tensor(out=m_rest[:], in0=m_rest[:], in1=mp[:, 1], op=ALU.subtract).then_inc(pool_chain, 1)
                pool.wait_ge(pool_chain, at_loop(k + 4, i, 8))
                plain_next()
                nc.gpsimd.tensor_copy(mp[:, 2], m_rest[:]).then_inc(m_split, 1)

            def zero_future(u, i):
                tiles = key_tiles(u)
                for t in range(QT * is_late(u), tiles):
                    pool.wait_ge(exp_done, at_loop(2 * (TILE0[u] + t) + 2, i, 4 * tiles))
                    plain_next()
                    d = probs[:, t % 4, :, 0:P]
                    nc.gpsimd.affine_select(out=d, in_=d, compare_op=ALU.is_ge, fill=0.0, base=0,
                                            pattern=[[0, UH], [1, P]], channel_multiplier=-1).then_inc(diag_done, 1)

            def step(n, i=None):
                if 1 <= n <= NU:
                    split_max(n, i)
                if n >= 2:
                    zero_future(n - 2, i)

            for c in range(NCH):
                step(UP * c)
                step(UP * c + 1)
                with pool.Fori(0, PAIRS - 1) as i:
                    for s in range(2):
                        step(UP * c + 2 + s, i)
            step(NU)
            step(NU + 1)

            def normalise(n, i):
                c = n // QT
                if n >= 2:
                    pool.wait_ge(y_full, at_loop(n - 1, i, 2))
                tok = bass.ds(at_loop((n % QT) * P, i, 2 * P), P)
                nc.gpsimd.tensor_tensor(out=att[:, n % 2], in0=heads_of(c)[:, :, tok], in1=rcps_of(c)[:, :, tok],
                                        op=ALU.mult).then_inc(att_ready, 1)

            def add_bias(n, i):
                pool.wait_ge(x1_ready, at_loop(n + 1, i, 2))
                if n >= 2:
                    pool.wait_ge(y_ready, at_loop(n - 1, i, 2))
                nc.gpsimd.tensor_tensor(out=x1b[:, n % 2], in0=x1[:, n % 2], in1=bias_sb[:], op=ALU.add).then_inc(x1b_ready, 1)

            def ffn_step(n, i=None):
                if n < NT:
                    normalise(n, i)
                if n:
                    add_bias(n - 1, i)

            pool.wait_ge(w2_in, 16 * N_W2)
            pool.wait_ge(heads_in[0], 16 * 4 * UH)
            for n in range(QT):
                ffn_step(n)
            for c in range(1, NCH):
                pool.wait_ge(heads_in[c], 16 * 4 * UH)
                with pool.Fori(0, QT // 2) as i:
                    for s in range(2):
                        ffn_step(QT * c + s, i)
            ffn_step(NT)


def constants():
    import numpy as np

    bf16 = np.dtype("bfloat16")

    def parts(a, n):
        out, rest = [], np.asarray(a, np.float64)
        for _ in range(n):
            out.append(rest.astype(np.float32).astype(bf16))
            rest = rest - out[-1].astype(np.float64)
        return out

    slopes = ((2.0 ** (-(2.0 ** (3 - np.log2(H))))) ** np.arange(1, H + 1)).astype(np.float32).astype(np.float64)
    pos = np.arange(S, dtype=np.float64)
    slope_rows = [np.broadcast_to(a[:, None], (H, S)) for a in parts(slopes, 3)]
    q_rows = np.stack(slope_rows + slope_rows + parts(-slopes[:, None] * pos[None, :], 4))
    one = np.ones(S)
    stairs = [DH * r for r in range(1, N_STAIR + 1)]
    k_rows = np.stack([pos % P] * 3 + [pos - pos % P] * 3 + [one] * 7 + [pos % P >= r for r in stairs]).astype(bf16)
    kmask = np.zeros((P, 3), np.float32)
    for n, (_, b) in enumerate(PARTS):
        kmask[DH * n:DH * (n + 1), b] = 1.0
    return {
        "ident": np.eye(P, dtype=np.float32),
        "identb": np.eye(P, dtype=np.float32).astype(bf16),
        "mneg": (np.triu(np.ones((P, P)), 1) * -1e30).astype(bf16),
        "kmask": kmask,
        "kalibi": k_rows,
        "qalibi": q_rows,
        "stair": np.tile([np.where(pos[:P] < r, -1e30, 0.0) for r in stairs], (1, H * QT)).astype(bf16),
        "iota": np.broadcast_to(np.arange(E, dtype=np.float32), (P, E)).copy(),
    }


def kernel(L0_attn_hidden_states, L0_attn_Wqkv, L0_attn_Wo, L0_ffn_W_base, L0_ffn_b_base, L0_ffn_W_gate, L0_ffn_A, L0_ffn_B):
    import numpy as np
    import concourse.bacc as bacc
    from concourse.bass_utils import run_bass_kernel_spmd as run

    w = np.asarray(L0_attn_Wqkv)
    arrays = {
        "x": np.asarray(L0_attn_hidden_states).reshape(B * S, D),
        "wqkv": np.concatenate([w[:, :D]] + [w[:, D:D + DH]] * len(PARTS) + [w[:, D + DH:]], axis=1),
        "wo": np.asarray(L0_attn_Wo),
        "wb": np.asarray(L0_ffn_W_base).T,
        "ag": np.concatenate([np.asarray(L0_ffn_A).reshape(E * R, D).T, np.asarray(L0_ffn_W_gate).T], axis=1),
        "lora": np.asarray(L0_ffn_B).transpose(0, 2, 1).reshape(E * R, D),
        "bias": np.broadcast_to(np.asarray(L0_ffn_b_base), (P, D)),
        **constants(),
    }
    nc = bacc.Bacc("TRN2", target_bir_lowering=False, num_devices=1)
    args, fed = [], {}
    for name, a in arrays.items():
        a = np.ascontiguousarray(a)
        fed[f"in_{name}"] = a
        args.append(nc.dram_tensor(f"in_{name}", a.shape, mybir.dt.from_np(a.dtype), kind="ExternalInput").ap())
    out = nc.dram_tensor("out", (B * S, D), F32, kind="ExternalOutput").ap()
    build(nc, *args, out)
    r = run(nc, [fed], core_ids=[0])
    return r.results[0]["out"].reshape(B, S, D)
```

```python
from contextlib import ExitStack

import concourse.bass as bass
from concourse import mybir

F32 = mybir.dt.float32
BF16 = mybir.dt.bfloat16
U32 = mybir.dt.uint32
ALU = mybir.AluOpType
ACT = mybir.ActivationFunctionType
AX_X = mybir.AxisListType.X

P = 128
B, S, D = 2, 1024, 512
H, DH = 32, 16
E, R = 8, 16
KC = D // P
CH = 512
QT = CH // P
NCH = B * S // CH
UH = 4
PAIRS = H // UH // 2
NB = 2 * PAIRS
NK = B * NB
NU = 2 * NK
PARTS = ((0, 0), (0, 1), (0, 2), (1, 0), (1, 1), (2, 0))
ROW_ALIBI = len(PARTS) * DH
N_ALIBI = 10
ROW_MAX = ROW_ALIBI + N_ALIBI
ROWS = ROW_MAX + 3
N_STAIR = P // DH - 1
STAIR_ROWS = ROWS + N_STAIR
QSCALE = DH ** -0.5
EPS = 1e-5
VW = 32
TURN_AFTER = 3
LAG = 2
XW = E * R + E
NT = B * S // P
LINKS_PER_TILE = 16


class Chain:

    def __init__(self, eng, sem):
        self.eng, self.sem, self.n, self.i, self.per = eng, sem, 0, None, 0

    def link(self, ins, plain_next=False):
        ins.then_inc(self.sem, 1)
        self.n += 1
        self.eng.wait_ge(self.sem, self.n if self.i is None else self.n + self.i * self.per)
        if plain_next:
            self.eng.nop(nofuse=True)

    def enter(self, i, per):
        self.i, self.per, self.first = i, per, self.n

    def leave(self, times):
        assert self.n - self.first == self.per
        self.n, self.i = self.first + times * self.per, None


def max_slots(late):
    out = []
    for t in range(QT):
        if late:
            out += [("full", late, t, (j,)) for j in range(UH)]
        per = 2 if t < 2 else 1
        out += [("diag", late, t, tuple(range(j, j + per))) for j in range(0, UH, per)]
    return out


EARLY_SLOTS = len(max_slots(0))
SLOTS = max_slots(0) + max_slots(1)
TURN = [EARLY_SLOTS + TURN_AFTER, len(SLOTS) + 1]
SLOTS.insert(TURN[0], ("turn", 0, None, None))
SLOTS.insert(TURN[1], ("turn", 1, None, None))
NSL = len(SLOTS)
NSB = 3
TILES = [(0, t, P * t) for t in range(QT)] + [(1, t, max(0, P * (t - QT))) for t in range(2 * QT)]
NTI = len(TILES)
DIAGS = 2 * QT
HALVES = [2 if CH - off > 256 else 1 for _, _, off in TILES]
SC0 = [sum(HALVES[:n]) for n in range(NTI + 1)]
NSC = SC0[NTI]


def pe_order(k):
    work = []
    for n, (late, t, off) in enumerate(TILES):
        w = CH - off
        if 1 <= k <= NK:
            work.append((UH // HALVES[n] * w, ("scores", k - 1, (n, 0))))
        m, v = (k - 1, n - LAG) if n >= LAG else (k - 2, n - LAG + NTI)
        if 0 <= m < NK:
            work.append((UH * (CH - TILES[v][2]), ("values", m, v)))
        if 1 <= k <= NK and HALVES[n] == 2:
            work.append((UH // 2 * w, ("scores", k - 1, (n, 1))))
        if k == NK + 1 and n == LAG - 1:
            break
    slots = [("slot", k, r) for r in range(NSL)] if k < NK else []
    total = sum(w for w, _ in work)
    out, done, put = [], 0, 0
    for w, piece in work:
        done += w
        upto = min(NSL - 1, round(NSL * done / (SLOTS_BY * total)))
        out += slots[put:upto]
        put = max(put, upto)
        out.append(piece)
    return out + slots[put:]


SLOTS_BY = 0.92
assert NSC % 2 == 0 and NSL % NSB == 0 and NTI % 4 == 0


def build(nc, x, wqkv, wo, wb, ag, lora, bias, ident_in, identb_in, mneg_in, kmask_in, kalibi_in, qalibi_in, stair_in, iota_in, out):
    with ExitStack() as ctx:
        def sb(name, shape, dt=F32):
            return ctx.enter_context(nc.sbuf_tensor(name, shape, dt))

        def sem(name):
            return ctx.enter_context(nc.semaphore(name))

        q_dram = nc.dram_tensor("q_dram", (NCH, 3, D, CH), BF16, kind="Internal").ap()
        m_dram = nc.dram_tensor("m_dram", (NU, 3, UH * QT, P), BF16, kind="Internal").ap()
        o_dram = nc.dram_tensor("o_dram", (NU, P, CH), F32, kind="Internal").ap()
        sum_dram = nc.dram_tensor("sum_dram", (NU, UH, CH), F32, kind="Internal").ap()
        rcp_dram = nc.dram_tensor("rcp_dram", (NU, UH, CH), F32, kind="Internal").ap()

        AR = PAIRS * CH
        arena = sb("arena", [P, 2 * AR * 2 + H * CH])
        q_op = arena[:, 4 * AR:4 * AR + H * CH].bitcast(BF16)
        q_op_pairs = q_op[:, :].rearrange("p (l g n) -> p l g n", g=PAIRS, l=2)

        def heads_of(c):
            return arena[:, c * 2 * AR:c * 2 * AR + AR].rearrange("p (g q) -> p g q", g=PAIRS)

        def rcps_of(c):
            return arena[:, c * 2 * AR + AR:(c + 1) * 2 * AR].rearrange("p (g q) -> p g q", g=PAIRS)

        work = sb("work", [P, 4 * UH * CH])
        probs = work[:, :].rearrange("p (r j q) -> p r j q", r=4, j=UH)
        xnT = work[:, 0:2 * KC * CH].rearrange("p (r k q) -> p r k q", r=2, k=KC)
        q4 = work[:, 4096:4096 + 2 * CH].rearrange("p (r q) -> p r q", r=2)
        qpart = work[:, 5120:5120 + 6 * CH].bitcast(BF16).rearrange("p (r a q) -> p r a q", r=4, a=3)
        k_tmp = sb("k_tmp", [P, 3 * CH + 3 * CH // 2])

        def x2_of(c):
            at = k_tmp[:, 0:QT * D] if c == 0 else work[:, (c - 1) * QT * D:c * QT * D]
            return at.rearrange("p (n d) -> p n d", d=D)

        x_sb = sb("x_sb", [P, 2, QT, D])
        k_op = sb("k_op", [P, B, S], BF16)
        v_op = sb("v_op", [P, B * S // P, 2, VW])
        wqkv_sb = sb("wqkv_sb", [P, KC, D + 112])
        wo_sb = sb("wo_sb", [P, KC, D])
        wb_sb = sb("wb_sb", [P, KC, D])
        ag_sb = sb("ag_sb", [P, KC, XW])
        lora_sb = sb("lora_sb", [P, D])
        bias_sb = sb("bias_sb", [P, D])
        ident = sb("ident", [P, P])
        identb = sb("identb", [P, P], BF16)
        mneg = sb("mneg", [P, P], BF16)
        kmask = sb("kmask", [P, 3])
        iota = sb("iota", [P, E])
        kv = k_tmp[0:112, 0:CH]
        k_rest = k_tmp[0:96, CH:2 * CH]
        k_sum = k_tmp[0:96, 2 * CH:3 * CH]
        k_part = k_tmp[0:96, 3 * CH:3 * CH + 3 * CH // 2].bitcast(BF16).rearrange("p (a q) -> p a q", a=3)
        stats = sb("stats", [P, QT, 6])
        mv = sb("mv", [P, QT, 2])
        ve = sb("ve", [P, QT])
        lnv = sb("lnv", [P, QT])
        rstd = sb("rstd", [P, QT])
        newt = sb("newt", [P, QT])
        negm = sb("negm", [P, 2, 2, UH * QT])
        m_t = sb("m_t", [UH * QT, 2, P])
        m_rest = sb("m_rest", [UH * QT, P])
        m_part = sb("m_part", [UH * QT, 2, 3, P], BF16)
        o_sb = sb("o_sb", [P, 2, CH])
        sums = sb("sums", [P, 2 * P])
        x1, x1b, xn2 = x_sb[:, 0, 0:2], x_sb[:, 0, 2:4], x_sb[:, 1, 0:2]
        xn2T = x_sb[:, 1, 2:4].rearrange("p r (k q) -> p r k q", k=KC)
        old_w = wqkv_sb[:, :, :].rearrange("p k n -> p (k n)")
        att = old_w[:, 0:2 * D].rearrange("p (r g q) -> p r g q", r=2, g=PAIRS)
        y_sb = old_w[:, 2 * D:4 * D].rearrange("p (r d) -> p r d", r=2)
        ff = sb("ff", [P, 2, 64])
        idx8 = sb("idx8", [P, 2, 8], U32)
        hw = sb("hw", [P, 2, E * R])
        hwT = sb("hwT", [P, 2, P])

        psum = ctx.enter_context(nc.psum_tensor("psum", [P, 8, 512], F32))

        w_in = sem("w_in")
        c_in = sem("c_in")
        w2_in = sem("w2_in")
        ones_set = sem("ones_set")
        x_in = [sem("x_in0"), sem("x_in1")]
        var_ready = sem("var_ready")
        ln_done = sem("ln_done")
        rstd_guess = sem("rstd_guess")
        xn_ready = sem("xn_ready")
        turned = sem("turned")
        xnT_ready = sem("xnT_ready")
        proj_full = sem("proj_full")
        proj_free = sem("proj_free")
        q_hi_ready = sem("q_hi_ready")
        q_split = sem("q_split")
        q_stored = sem("q_stored")
        vt_full = sem("vt_full")
        v_ready = sem("v_ready")
        k_ready = sem("k_ready")
        dve_chain = sem("dve_chain")
        q_loaded = sem("q_loaded")
        slot_full = sem("slot_full")
        slot_free = sem("slot_free")
        max_late = sem("max_late")
        pool_chain = sem("pool_chain")
        m_split = sem("m_split")
        m_stored = sem("m_stored")
        m_loaded = sem("m_loaded")
        s_full = sem("s_full")
        exp_done = sem("exp_done")
        diag_done = sem("diag_done")
        pv_done = sem("pv_done")
        o_copied = sem("o_copied")
        o_stored = sem("o_stored")
        sums_in = sem("sums_in")
        rcp_ready = sem("rcp_ready")
        rcp_stored = sem("rcp_stored")
        heads_in = [sem(f"heads_in{c}") for c in range(NCH)]
        x2_in = [sem(f"x2_in{c}") for c in range(NCH)]
        att_ready = sem("att_ready")
        y_full = sem("y_full")
        x1_ready = sem("x1_ready")
        var2_ready = sem("var2_ready")
        ln2_done = sem("ln2_done")
        guess2 = sem("guess2")
        xn2_ready = sem("xn2_ready")
        x1b_ready = sem("x1b_ready")
        turned2 = sem("turned2")
        xn2T_ready = sem("xn2T_ready")
        h_full = sem("h_full")
        gap_ready = sem("gap_ready")
        e2_ready = sem("e2_ready")
        hw_ready = sem("hw_ready")
        hw_turned = sem("hw_turned")
        hwT_ready = sem("hwT_ready")
        z_full = sem("z_full")
        y_ready = sem("y_ready")
        out_sem = [sem("out_sem0"), sem("out_sem1")]

        block = ctx.enter_context(nc.Block())
        x_rows = x.rearrange("(c t p) d -> c p t d", t=QT, p=P)
        out_rows = out.rearrange("(n p) d -> n p d", p=P)
        N_W, N_C, N_W2 = 6, 8, 5

        def at_loop(base, i, per):
            return base if i is None else base + i * per

        def unit_col(u, j, i):
            g, s = (u % (2 * NB)) // 4, (u // 2) % 2
            return at_loop((((PAIRS * (u % 2) + g) * 2 + s) * UH + j) * CH, i, 2 * UH * CH)

        @block.sync
        def _(sp):
            for t in range(QT):
                sp.dma_start(x_sb[:, 0, t], x_rows[0][:, t]).then_inc(x_in[0], 16)
            sp.dma_start(x_sb[:, 1], x_rows[1]).then_inc(x_in[1], 16)
            sp.dma_start(identb[:], identb_in).then_inc(c_in, 16)
            sp.dma_start(mneg[:], mneg_in).then_inc(c_in, 16)
            for b in range(B):
                sp.dma_start(k_op[ROW_ALIBI:STAIR_ROWS, b, :], kalibi_in).then_inc(c_in, 16)
            sp.dma_start(q_op[ROW_ALIBI:ROW_MAX, :], qalibi_in).then_inc(c_in, 16)
            for a in range(2):
                sp.dma_start(q_op[ROWS:STAIR_ROWS, a * H * CH:(a + 1) * H * CH], stair_in).then_inc(c_in, 16)
            sp.dma_start(iota[:], iota_in).then_inc(c_in, 16)
            for c in (2, 3):
                sp.wait_ge(turned, QT * (c - 1))
                sp.dma_start(x_sb[:, c % 2], x_rows[c]).then_inc(x_in[c % 2], 16)
            sp.dma_start(wo_sb[:], wo.rearrange("(k p) n -> p k n", p=P)).then_inc(w2_in, 16)
            sp.dma_start(wb_sb[:], wb.rearrange("(k p) n -> p k n", p=P)).then_inc(w2_in, 16)
            sp.dma_start(ag_sb[:], ag.rearrange("(k p) n -> p k n", p=P)).then_inc(w2_in, 16)
            sp.dma_start(lora_sb[:], lora).then_inc(w2_in, 16)
            sp.dma_start(bias_sb[:], bias).then_inc(w2_in, 16)

            def load_queries(c):
                sp.wait_ge(q_loaded, 16 * 6 * c)
                sp.wait_ge(q_stored, 16 * 4 * (c + 1))
                for n, (a, _) in enumerate(PARTS):
                    sp.dma_start(q_op_pairs[DH * n:DH * (n + 1), c % 2].rearrange("d g (h q) -> d (g h) q", q=CH),
                                 q_dram[c, a].rearrange("(h d) q -> d h q", d=DH)).then_inc(q_loaded, 16)

            def load_pair(g, i=None):
                sp.wait_ge(q_loaded, at_loop(16 * 12 * (1 + g), i, 16 * 12))
                plain_next()
                sp.wait_ge(s_full, at_loop(NSC * 2 * (g + 1), i, 2 * NSC))
                plain_next()
                gi = at_loop(g, i, 1)
                for late in range(2):
                    for n, (a, _) in enumerate(PARTS):
                        sp.dma_start(q_op_pairs[DH * n:DH * (n + 1), late, bass.ds(gi, 1)].rearrange("d g (h q) -> d (g h) q", q=CH),
                                     q_dram[NCH // 2 + late, a, bass.ds(gi * P, P)].rearrange("(h d) q -> d h q", d=DH)
                                     ).then_inc(q_loaded, 16)

            def plain_next():
                sp.nop(nofuse=True)

            def store_unit(u, i=None):
                uu = at_loop(u, i, 4)
                sp.wait_ge(o_copied, at_loop(u + 1, i, 4))
                plain_next()
                if u:
                    sp.wait_ge(o_stored, at_loop(32 * u, i, 128))
                    plain_next()
                sp.dma_start(o_dram[bass.ds(uu, 1)].rearrange("u p q -> (u p) q"), o_sb[:, u % 2]).then_inc(o_stored, 16)
                ones = DH * (1 - (u // 2) % 2)
                sp.dma_start(sum_dram[bass.ds(uu, 1)].rearrange("u j q -> (u j) q"),
                             o_sb[ones:P:VW, u % 2]).then_inc(o_stored, 16)

            def max_rows(u, i=None):
                uu = at_loop(u, i, 4)
                sp.wait_ge(m_split, at_loop(u + 1, i, 4))
                plain_next()
                sp.dma_start(m_dram[bass.ds(uu, 1)].rearrange("u a n q -> n (u a) q"), m_part[:, u % 2]).then_inc(m_stored, 16)
                sp.wait_ge(m_stored, at_loop(16 * (u + 1), i, 64))
                plain_next()
                if u:
                    sp.wait_ge(m_loaded, at_loop(16 * u, i, 64))
                    plain_next()
                sp.dma_start(q_op[ROW_MAX:ROWS, bass.ds(unit_col(u, 0, i), UH * CH)],
                             m_dram[bass.ds(uu, 1)].rearrange("u a n q -> (u a) (n q)")).then_inc(m_loaded, 16)

            def load_sums(b):
                sp.wait_ge(o_stored, 32 * 2 * NB * (b + 1))
                if b:
                    sp.wait_ge(rcp_stored, 16 * b)
                sp.dma_start(sums[:], sum_dram[2 * NB * b:2 * NB * (b + 1)].rearrange("u j (s q) -> (u j s) q", s=2)
                             ).then_inc(sums_in, 16)

            def store_rcps(b):
                sp.wait_ge(rcp_ready, b + 1)
                sp.dma_start(rcp_dram[2 * NB * b:2 * NB * (b + 1)].rearrange("u j (s q) -> (u j s) q", s=2), sums[:]
                             ).then_inc(rcp_stored, 16)

            def load_heads(c):
                b = c // 2
                sp.wait_ge(rcp_stored, 16 * (b + 1))
                units = slice(2 * NB * b, 2 * NB * (b + 1))
                o_c = o_dram[units].rearrange("(g s l) p q -> l s p g q", s=2, l=2)[c % 2]
                r_c = rcp_dram[units].rearrange("(g s l) j q -> l s j g q", s=2, l=2)[c % 2]
                for j in range(UH):
                    for s in range(2):
                        p0 = VW * j + DH * s
                        sp.dma_start(heads_of(c)[p0:p0 + DH], o_c[s, p0:p0 + DH]).then_inc(heads_in[c], 16)
                        sp.dma_start(rcps_of(c)[p0:p0 + DH],
                                     r_c[s, j:j + 1].broadcast_to((DH, PAIRS, CH))).then_inc(heads_in[c], 16)

            def step(k, i=None):
                if k >= 2:
                    store_unit(2 * k - 3, i)
                if k < NK:
                    max_rows(2 * k, i)
                if 1 <= k <= NK:
                    store_unit(2 * k - 2, i)
                if k < NK:
                    max_rows(2 * k + 1, i)

            load_queries(0)
            load_queries(1)
            sp.wait_ge(k_ready, NCH)
            sp.wait_ge(v_ready, NCH)
            sp.dma_start(x2_of(0), x_rows[0]).then_inc(x2_in[0], 16)
            step(0)
            step(1)
            with sp.Fori(0, PAIRS - 1) as i:
                step(2, i)
                load_pair(0, i)
                step(3, i)
            step(NB)
            load_pair(PAIRS - 1)
            step(NB + 1)
            load_sums(0)
            with sp.Fori(0, PAIRS - 1) as i:
                step(NB + 2, i)
                step(NB + 3, i)
            store_rcps(0)
            store_unit(2 * NK - 3)
            load_heads(0)
            store_unit(2 * NK - 2)
            load_heads(1)
            step(NK + 1)
            sp.wait_ge(pv_done, NTI * NK)
            load_sums(1)
            sp.dma_start(x2_of(1), x_rows[1]).then_inc(x2_in[1], 16)
            store_rcps(1)
            for c in (2, 3):
                load_heads(c)
                sp.dma_start(x2_of(c), x_rows[c]).then_inc(x2_in[c], 16)
            with sp.Fori(0, NT // 2) as i:
                for s in range(2):
                    sp.wait_ge(y_ready, i * 2 + s + 1)
                    plain_next()
                    sp.dma_start(out_rows[bass.ds(i * 2 + s, 1)].rearrange("n p d -> (n p) d"), y_sb[:, s]).then_inc(out_sem[s], 16)
            for s in range(2):
                sp.wait_ge(out_sem[s], 16 * (NT // 2))

        @block.tensor
        def _(pe):
            pe.wait_ge(w_in, 16 * N_W)

            def transposes(c):
                for t in range(QT):
                    n = QT * c + t
                    pe.wait_ge(xn_ready, n + 1)
                    if n >= 2:
                        pe.wait_ge(xnT_ready, n - 1)
                    for k in range(KC):
                        last = nc.tensor.transpose(psum[:, n % 2, k * P:(k + 1) * P],
                                                   x_sb[:, c % 2, t, k * P:(k + 1) * P], ident[:])
                    last.then_inc(turned, 1)

            def project(c, m):
                if m == 0:
                    pe.wait_ge(xnT_ready, QT * (c + 1))
                if c:
                    pe.wait_ge(proj_free, 5 * (c - 1) + m + 1)
                width = P if m < 4 else 112
                for k in range(KC):
                    last = nc.tensor.matmul(psum[0:width, 2 + m, :], wqkv_sb[:, k, P * m:P * m + width], xnT[:, c % 2, k, :],
                                            start=(k == 0), stop=(k == KC - 1))
                last.then_inc(proj_full, 1)

            def values(c):
                pe.wait_ge(proj_free, 5 * c + 5)
                if c:
                    pe.wait_ge(v_ready, c)
                for t in range(QT):
                    last = nc.tensor.transpose(psum[:, 7, 112 * t:112 * (t + 1)], kv[:, t * P:(t + 1) * P], ident[0:112, 0:112])
                last.then_inc(vt_full, 1)

            transposes(0)
            for c in range(NCH):
                for m in range(5):
                    project(c, m)
                    if m == 0 and c:
                        values(c - 1)
                    if m == 2 and c + 1 < NCH:
                        transposes(c + 1)
            values(NCH - 1)

            def max_slot(k, r, i):
                kind, late, t, js = SLOTS[r]
                idx, per = NSL * k + r, 2 * NSL
                if idx >= NSB:
                    pe.wait_ge(slot_free, at_loop(idx - NSB + 1, i, per))
                bank = psum[:, idx % NSB]
                if kind == "turn":
                    if late:
                        pe.wait_ge(max_late, at_loop(k + 1, i, 2))
                    else:
                        pe.wait_ge(slot_free, at_loop(NSL * k + EARLY_SLOTS, i, per))
                    nc.tensor.transpose(bank[0:UH * QT, 0:P], negm[:, late, 0, :], ident[:]).then_inc(slot_full, 1)
                    return
                b = k // NB
                width = P * (t + 1) if kind == "diag" else CH
                k0 = CH * late if kind == "diag" else 0
                for a, j in enumerate(js):
                    col = unit_col(2 * k + late, j, i) + t * P
                    last = nc.tensor.matmul(bank[:, a * width:(a + 1) * width], q_op[0:ROW_MAX, bass.ds(col, P)],
                                            k_op[0:ROW_MAX, b, k0:k0 + width],
                                            start=(a == 0), stop=(kind == "full"), skip_group_check=True)
                if kind == "diag":
                    w = len(js) * width
                    masked = bank[:, 0:w].rearrange("p (a k) -> p a k", a=len(js))[:, :, width - P:width]
                    last = nc.tensor.matmul(masked, identb[:], mneg[:, None, :].broadcast_to((P, len(js), P)),
                                            start=False, stop=True, skip_group_check=True)
                last.then_inc(slot_full, 1)

            def scores(m, at, i):
                n, hp = at
                late, t, off = TILES[n]
                b, w = m // NB, CH - off
                if t == 0 and hp == 0:
                    pe.wait_ge(m_loaded, at_loop(16 * (2 * m + late + 1), i, 64))
                heads = UH // HALVES[n]
                idx = NSC * m + SC0[n] + hp
                if idx >= 2:
                    pe.wait_ge(exp_done, at_loop(idx - 1, i, 2 * NSC))
                for a in range(heads):
                    col = unit_col(2 * m + late, heads * hp + a, i) + off
                    at = psum[:, NSB + 2 * (idx % 2) + (a if heads == 2 else a * w // CH)]
                    at = at[:, 0:w] if heads == 2 else at[:, a * w % CH:a * w % CH + w]
                    diag = P if t >= QT * late else 0
                    if diag:
                        last = nc.tensor.matmul(at[:, 0:P], k_op[0:STAIR_ROWS, b, t * P:(t + 1) * P],
                                                q_op[0:STAIR_ROWS, bass.ds(col, P)], start=True, stop=True)
                    if diag < w:
                        last = nc.tensor.matmul(at[:, diag:w], k_op[0:ROWS, b, t * P:(t + 1) * P],
                                                q_op[0:ROWS, bass.ds(col + diag, w - diag)], start=True, stop=True)
                last.then_inc(s_full, 1)

            def values_product(m, n, i):
                late, t, off = TILES[n]
                b, u = m // NB, 2 * m + late
                if t == 0 and u:
                    pe.wait_ge(o_copied, at_loop(u, i, 4))
                pe.wait_ge(exp_done, at_loop(NSC * m + SC0[n + 1], i, 2 * NSC))
                if t >= QT * late:
                    pe.wait_ge(diag_done, at_loop(DIAGS * m + QT * late + t - QT * late + 1, i, 2 * DIAGS))
                last_tile = QT * (1 + late) - 1
                for j in range(UH):
                    last = nc.tensor.matmul(psum[VW * j:VW * (j + 1), 7, off:CH], v_op[:, b * (S // P) + t, m % 2, :],
                                            probs[:, n % 4, j, 0:CH - off], start=(t == 0), stop=(t == last_tile))
                last.then_inc(pv_done, 1)

            def step(k, i=None):
                for what, m, n in pe_order(k):
                    {"slot": max_slot, "scores": scores, "values": values_product}[what](m, n, i)

            pe.wait_ge(c_in, 16 * N_C)
            pe.wait_ge(v_ready, NCH)
            pe.wait_ge(k_ready, NCH)
            pe.wait_ge(q_loaded, 16 * 6 * 2)
            for b in range(B):
                if b:
                    pe.wait_ge(q_loaded, 16 * 12 * PAIRS)
                step(NB * b)
                step(NB * b + 1)
                if b:
                    pe.wait_ge(q_loaded, 16 * 12 * (1 + PAIRS))
                with pe.Fori(0, PAIRS - 1) as i:
                    step(NB * b + 2, i)
                    step(NB * b + 3, i)
            step(NK)
            step(NK + 1)

            pe.wait_ge(w2_in, 16 * N_W2)

            def out_proj(n, i):
                pe.wait_ge(att_ready, at_loop(n + 1, i, 2))
                if n >= 2:
                    pe.wait_ge(x1_ready, at_loop(n - 1, i, 2))
                for g in range(PAIRS):
                    last = nc.tensor.matmul(psum[:, n % 2], att[:, n % 2, g, :], wo_sb[:, g, :], start=(g == 0), stop=(g == PAIRS - 1))
                last.then_inc(y_full, 1)

            def turn_xn2(n, i):
                pe.wait_ge(xn2_ready, at_loop(n + 1, i, 2))
                if n >= 2:
                    pe.wait_ge(xn2T_ready, at_loop(n - 1, i, 2))
                for k in range(KC):
                    last = nc.tensor.transpose(psum[:, 2 + n % 2, k * P:(k + 1) * P], xn2[:, n % 2, k * P:(k + 1) * P], ident[:])
                last.then_inc(turned2, 1)

            def base_and_lora_in(n, i):
                pe.wait_ge(xn2T_ready, at_loop(n + 1, i, 2))
                if n >= 1:
                    pe.wait_ge(hw_ready, at_loop(n, i, 2))
                for k in range(KC):
                    last = nc.tensor.matmul(psum[:, 4, 0:XW], xn2T[:, n % 2, k, :], ag_sb[:, k, :], start=(k == 0), stop=(k == KC - 1))
                last.then_inc(h_full, 1)
                if n >= 2:
                    pe.wait_ge(y_ready, at_loop(n - 1, i, 2))
                for k in range(KC):
                    nc.tensor.matmul(psum[:, 6 + n % 2], xn2T[:, n % 2, k, :], wb_sb[:, k, :], start=(k == 0), stop=False)

            def turn_hw(n, i):
                pe.wait_ge(hw_ready, at_loop(n + 1, i, 2))
                if n >= 1:
                    pe.wait_ge(hwT_ready, at_loop(n, i, 2))
                nc.tensor.transpose(psum[:, 5, 0:P], hw[:, n % 2], ident[:]).then_inc(hw_turned, 1)

            def lora_out(n, i):
                pe.wait_ge(hwT_ready, at_loop(n + 1, i, 2))
                nc.tensor.matmul(psum[:, 6 + n % 2], hwT[:, n % 2], lora_sb[:], start=False, stop=True).then_inc(z_full, 1)

            def ffn_step(n, i=None):
                if n < NT:
                    out_proj(n, i)
                if 1 <= n <= NT:
                    turn_xn2(n - 1, i)
                if 2 <= n:
                    turn_hw(n - 2, i)
                if 1 <= n <= NT:
                    base_and_lora_in(n - 1, i)
                if 2 <= n:
                    lora_out(n - 2, i)

            for n in range(QT):
                ffn_step(n)
            for c in range(1, NCH):
                with pe.Fori(0, QT // 2) as i:
                    for s in range(2):
                        ffn_step(QT * c + s, i)
            ffn_step(NT)
            ffn_step(NT + 1)

        @block.scalar
        def _(act):
            def rstd_first(c):
                act.wait_ge(var_ready, c + 1)
                nc.scalar.activation(lnv[:], ve[:], ACT.Ln).then_inc(ln_done, 1)
                act.wait_ge(ln_done, c + 1)
                nc.scalar.activation(rstd[:], lnv[:], ACT.Exp, scale=-0.5).then_inc(rstd_guess, 1)

            def xnT_copies(c):
                for t in range(QT):
                    n = QT * c + t
                    act.wait_ge(turned, n + 1)
                    if t == 0 and c >= 2:
                        act.wait_ge(proj_full, 5 * (c - 1))
                    nc.scalar.copy(xnT[:, c % 2, :, t * P:(t + 1) * P],
                                   psum[:, n % 2].rearrange("p (k q) -> p k q", k=KC)).then_inc(xnT_ready, 1)

            def query_hi(c, m):
                n = 4 * c + m
                act.wait_ge(proj_full, 5 * c + m + 1)
                if n >= 2:
                    act.wait_ge(q_split, n - 1)
                if n >= 4:
                    act.wait_ge(q_stored, 16 * (n - 3))
                nc.scalar.mul(q4[:, n % 2], psum[:, 2 + m], QSCALE).then_inc(proj_free, 1)
                act.wait_ge(proj_free, 5 * c + m + 1)
                nc.scalar.copy(qpart[:, n % 4, 0], q4[:, n % 2]).then_inc(q_hi_ready, 1)

            def keys_values(c):
                act.wait_ge(proj_full, 5 * c + 5)
                if c:
                    act.wait_ge(k_ready, c)
                    act.wait_ge(vt_full, c)
                nc.scalar.copy(kv[:], psum[0:112, 6]).then_inc(proj_free, 1)

            act.dma_start(ident[:], ident_in).then_inc(w_in, 16)
            act.dma_start(kmask[:], kmask_in).then_inc(w_in, 16)
            for k in range(KC):
                act.dma_start(wqkv_sb[:, k], wqkv[P * k:P * (k + 1)]).then_inc(w_in, 16)
            act.preload_act_table_set("natural_log_exp_and_others")
            rstd_first(0)
            xnT_copies(0)
            rstd_first(1)
            for c in range(NCH):
                for m in range(4):
                    query_hi(c, m)
                    if m == 2 and c + 1 < NCH:
                        xnT_copies(c + 1)
                keys_values(c)
                if c + 2 < NCH:
                    rstd_first(c + 2)

            def exps(m, n, i):
                w = CH - TILES[n][2]
                if NTI * m + n >= 4:
                    act.wait_ge(pv_done, at_loop(NTI * m + n - 3, i, 2 * NTI))
                heads = UH // HALVES[n]
                for hp in range(HALVES[n]):
                    idx = NSC * m + SC0[n] + hp
                    act.wait_ge(s_full, at_loop(idx + 1, i, 2 * NSC))
                    b0 = NSB + 2 * (idx % 2)
                    if heads == 2:
                        src = psum[:, b0:b0 + 2, 0:w]
                    else:
                        src = psum[:, b0:b0 + 2].rearrange("p b q -> p (b q)")[:, 0:UH * w].rearrange("p (j q) -> p j q", j=UH)
                    nc.scalar.activation(probs[:, n % 4, heads * hp:heads * (hp + 1), 0:w], src, ACT.Exp).then_inc(exp_done, 1)
                    if hp == 0 and n == LAG - 1 and m:
                        copy_unit(2 * m - 1, i)
                    if hp == 0 and n == QT + LAG - 1:
                        copy_unit(2 * m, i)

            def copy_unit(u, i=None):
                act.wait_ge(pv_done, at_loop(NTI * (u // 2) + (NTI if u % 2 else QT), i, 2 * NTI))
                if u >= 2:
                    act.wait_ge(o_stored, at_loop(32 * (u - 1), i, 128))
                nc.scalar.copy(o_sb[:, u % 2], psum[:, 7]).then_inc(o_copied, 1)

            def step(k, i=None):
                m = k - 1
                for n in range(NTI):
                    exps(m, n, i)

            act.wait_ge(q_stored, 16 * 4 * NCH)
            step(1)
            for b in range(B):
                if b:
                    step(NB * b)
                    step(NB * b + 1)
                with act.Fori(0, PAIRS - 1) as i:
                    step(NB * b + 2, i)
                    step(NB * b + 3, i)
            step(NK)
            copy_unit(NU - 1)

            def guess(n, i):
                act.wait_ge(var2_ready, at_loop(n + 1, i, 2))
                nc.scalar.activation(ff[:, n % 2, 2:3], ff[:, n % 2, 1:2], ACT.Ln).then_inc(ln2_done, 1)
                act.wait_ge(ln2_done, at_loop(n + 1, i, 2))
                nc.scalar.activation(ff[:, n % 2, 3:4], ff[:, n % 2, 2:3], ACT.Exp, scale=-0.5).then_inc(guess2, 1)

            def copy_xn2T(n, i):
                act.wait_ge(turned2, at_loop(n + 1, i, 2))
                if n >= 2:
                    act.wait_ge(z_full, at_loop(n - 1, i, 2))
                nc.scalar.copy(xn2T[:, n % 2], psum[:, 2 + n % 2].rearrange("p (k q) -> p k q", k=KC)).then_inc(xn2T_ready, 1)

            def second_weight(n, i):
                act.wait_ge(gap_ready, at_loop(n + 1, i, 2))
                nc.scalar.activation(ff[:, n % 2, 6:7], ff[:, n % 2, 5:6], ACT.Exp).then_inc(e2_ready, 1)

            def copy_hwT(n, i):
                act.wait_ge(hw_turned, at_loop(n + 1, i, 2))
                if n >= 2:
                    act.wait_ge(z_full, at_loop(n - 1, i, 2))
                nc.scalar.copy(hwT[:, n % 2], psum[:, 5, 0:P]).then_inc(hwT_ready, 1)

            def ffn_step(n, i=None):
                if 1 <= n <= NT:
                    copy_xn2T(n - 1, i)
                if 2 <= n:
                    copy_hwT(n - 2, i)
                if n < NT:
                    guess(n, i)
                if 1 <= n <= NT:
                    second_weight(n - 1, i)

            for n in range(QT):
                ffn_step(n)
            for c in range(1, NCH):
                with act.Fori(0, QT // 2) as i:
                    for s in range(2):
                        ffn_step(QT * c + s, i)
            ffn_step(NT)
            ffn_step(NT + 1)

        @block.vector
        def _(dve):
            chain = Chain(dve, dve_chain)
            link = chain.link

            nc.vector.memset(v_op[:], 1.0).then_inc(ones_set, 1)

            def newton(r, v, t):
                link(nc.vector.tensor_tensor(t, r, r, ALU.mult))
                link(nc.vector.tensor_tensor(t, t, v, ALU.mult))
                link(nc.vector.tensor_scalar(t, t, -0.5, 1.5, ALU.mult, ALU.add))
                link(nc.vector.tensor_tensor(r, r, t, ALU.mult))

            def norm(c):
                dve.wait_ge(x_in[c % 2], 16 * {0: QT, 1: 1, 2: QT + 1, 3: 2}[c])
                for t in range(QT):
                    last = nc.vector.bn_stats(stats[:, t], x_sb[:, c % 2, t])
                link(last)
                for t in range(QT):
                    last = nc.vector.bn_aggr(mv[:, t], stats[:, t])
                link(last)
                nc.vector.tensor_scalar(ve[:], mv[:, :, 1], EPS, None, ALU.add).then_inc(var_ready, 1)
                dve.wait_ge(rstd_guess, c + 1)
                dve.wait_ge(var_ready, c + 1)
                newton(rstd[:], ve[:], newt[:])
                for t in range(QT):
                    nc.vector.tensor_scalar(x_sb[:, c % 2, t], x_sb[:, c % 2, t], mv[:, t, 0:1], rstd[:, t:t + 1],
                                            ALU.subtract, ALU.mult).then_inc(xn_ready, 1)

            def split_queries(c):
                for m in range(4):
                    n = 4 * c + m
                    dve.wait_ge(q_hi_ready, n + 1)
                    link(nc.vector.tensor_tensor(q4[:, n % 2], q4[:, n % 2], qpart[:, n % 4, 0], ALU.subtract))
                    link(nc.vector.tensor_copy(qpart[:, n % 4, 1], q4[:, n % 2]))
                    nc.vector.tensor_tensor(qpart[:, n % 4, 2], q4[:, n % 2], qpart[:, n % 4, 1], ALU.subtract).then_inc(q_split, 1)

            def split_keys(c):
                dve.wait_ge(proj_free, 5 * c + 5)
                link(nc.vector.tensor_copy(k_part[:, 0], kv[0:96]))
                link(nc.vector.tensor_tensor(k_rest[:], kv[0:96], k_part[:, 0], ALU.subtract))
                link(nc.vector.tensor_copy(k_part[:, 1], k_rest[:]))
                link(nc.vector.tensor_tensor(k_part[:, 2], k_rest[:], k_part[:, 1], ALU.subtract))
                link(nc.vector.tensor_scalar(k_sum[:], k_part[:, 0], kmask[0:96, 0:1], None, ALU.mult))
                link(nc.vector.scalar_tensor_tensor(k_sum[:], k_part[:, 1], kmask[0:96, 1:2], k_sum[:], ALU.mult, ALU.add))
                nc.vector.scalar_tensor_tensor(k_op[0:96, c // 2, (c % 2) * CH:(c % 2 + 1) * CH], k_part[:, 2],
                                               kmask[0:96, 2:3], k_sum[:], ALU.mult, ALU.add).then_inc(k_ready, 1)

            def copy_values(c):
                dve.wait_ge(vt_full, c + 1)
                v = psum[:, 7, 0:QT * 112].rearrange("p (t n) -> p t n", t=QT)[:, :, 96:112]
                nc.vector.tensor_copy(v_op[:, QT * c:QT * (c + 1), 0, 0:DH], v)
                nc.vector.tensor_copy(v_op[:, QT * c:QT * (c + 1), 1, DH:VW], v).then_inc(v_ready, 1)

            dve.wait_ge(ones_set, 1)
            norm(0)
            norm(1)
            dve.wait_ge(w_in, 16 * N_W)
            for c in range(NCH):
                split_queries(c)
                split_keys(c)
                if c + 2 < NCH:
                    norm(c + 2)
                copy_values(c)

            def step(k, i=None):
                for r, (kind, late, t, js) in enumerate(SLOTS):
                    idx = NSL * k + r
                    if kind == "turn":
                        u = 2 * k + late
                        if late:
                            dve.wait_ge(slot_free, at_loop(idx, i, 2 * NSL))
                            nc.vector.tensor_tensor(negm[:, 1, 0, :], negm[:, 1, 0, :], negm[:, 1, 1, :], ALU.min
                                                    ).then_inc(max_late, 1)
                        dve.wait_ge(slot_full, at_loop(idx + 1, i, 2 * NSL))
                        if u >= 2:
                            dve.wait_ge(m_split, at_loop(u - 1, i, 4))
                        nc.vector.tensor_copy(m_t[:, u % 2], psum[0:UH * QT, idx % NSB, 0:P]).then_inc(slot_free, 1)
                        continue
                    dve.wait_ge(slot_full, at_loop(idx + 1, i, 2 * NSL))
                    width = P * (t + 1) if kind == "diag" else CH
                    where = 1 if kind == "full" else 0
                    dst = negm[:, late, where, :].rearrange("p (j t) -> p j t", t=QT)[:, js[0]:js[-1] + 1, t]
                    nc.vector.tensor_reduce(dst, psum[:, idx % NSB, 0:len(js) * width].rearrange("p (a k) -> p a k", a=len(js)),
                                            AX_X, ALU.max, negate=True).then_inc(slot_free, 1)

            def reciprocals(b):
                dve.wait_ge(sums_in, 16 * (b + 1))
                nc.vector.reciprocal(sums[:], sums[:]).then_inc(rcp_ready, 1)

            for b in range(B):
                step(NB * b)
                step(NB * b + 1)
                with dve.Fori(0, PAIRS - 1) as i:
                    step(NB * b + 2, i)
                    step(NB * b + 3, i)
            reciprocals(0)

            def residual(n, i):
                dve.wait_ge(y_full, at_loop(n + 1, i, 2))
                if n >= 2:
                    dve.wait_ge(x1b_ready, at_loop(n - 1, i, 2))
                nc.vector.tensor_tensor(x1[:, n % 2], x2_of(n // QT)[:, bass.ds(at_loop(n % QT, i, 2), 1)].rearrange("p n d -> p (n d)"), psum[:, n % 2], ALU.add).then_inc(x1_ready, 1)
                dve.wait_ge(x1_ready, at_loop(n + 1, i, 2))
                link(nc.vector.bn_stats(stats[:, n % 2], x1[:, n % 2]), plain_next=True)
                link(nc.vector.bn_aggr(mv[:, n % 2], stats[:, n % 2]))
                nc.vector.tensor_scalar(ff[:, n % 2, 1:2], mv[:, n % 2, 1:2], EPS, None, ALU.add).then_inc(var2_ready, 1)

            def norm2(n, i):
                dve.wait_ge(guess2, at_loop(n + 1, i, 2))
                newton(ff[:, n % 2, 3:4], ff[:, n % 2, 1:2], ff[:, n % 2, 4:5])
                if n >= 2:
                    dve.wait_ge(turned2, at_loop(n - 1, i, 2))
                nc.vector.tensor_scalar(xn2[:, n % 2], x1[:, n % 2], mv[:, n % 2, 0:1], ff[:, n % 2, 3:4],
                                        ALU.subtract, ALU.mult).then_inc(xn2_ready, 1)

            def route_first(n, i):
                f = ff[:, n % 2]
                dve.wait_ge(h_full, at_loop(n + 1, i, 2))
                link(nc.vector.tensor_copy(f[:, 8:16], psum[:, 4, E * R:XW]), plain_next=True)
                link(nc.vector.max(f[:, 16:24], f[:, 8:16]), plain_next=True)
                link(nc.vector.max_index(idx8[:, n % 2], f[:, 16:24], f[:, 8:16]))
                link(nc.vector.tensor_copy(f[:, 24:32], idx8[:, n % 2]))
                nc.vector.tensor_tensor(f[:, 5:6], f[:, 17:18], f[:, 16:17], ALU.subtract).then_inc(gap_ready, 1)

            def route_second(n, i):
                f = ff[:, n % 2]
                dve.wait_ge(e2_ready, at_loop(n + 1, i, 2))
                link(nc.vector.tensor_scalar(f[:, 7:8], f[:, 6:7], 1.0, None, ALU.add))
                link(nc.vector.reciprocal(f[:, 32:33], f[:, 7:8]))
                link(nc.vector.tensor_tensor(f[:, 33:34], f[:, 32:33], f[:, 6:7], ALU.mult))
                link(nc.vector.tensor_scalar(f[:, 40:48], iota[:], f[:, 24:25], f[:, 32:33], ALU.is_equal, ALU.mult))
                link(nc.vector.tensor_scalar(f[:, 48:56], iota[:], f[:, 25:26], f[:, 33:34], ALU.is_equal, ALU.mult))
                link(nc.vector.tensor_tensor(f[:, 56:64], f[:, 40:48], f[:, 48:56], ALU.add))
                if n >= 2:
                    dve.wait_ge(hw_turned, at_loop(n - 1, i, 2))
                nc.vector.tensor_tensor(hw[:, n % 2].rearrange("p (e r) -> p e r", e=E),
                                        psum[:, 4, 0:E * R].rearrange("p (e r) -> p e r", e=E),
                                        f[:, 56:64, None].broadcast_to((P, E, R)), ALU.mult).then_inc(hw_ready, 1)

            def finish(n, i):
                dve.wait_ge(z_full, at_loop(n + 1, i, 2))
                dve.wait_ge(x1b_ready, at_loop(n + 1, i, 2))
                if n >= 2:
                    dve.wait_ge(out_sem[n % 2], at_loop(16 * (n // 2), i, 16))
                nc.vector.tensor_tensor(y_sb[:, n % 2], x1b[:, n % 2], psum[:, 6 + n % 2], ALU.add).then_inc(y_ready, 1)

            def ffn_step(n, i=None):
                if n < NT:
                    residual(n, i)
                if 1 <= n <= NT:
                    route_first(n - 1, i)
                if n < NT:
                    norm2(n, i)
                if 1 <= n <= NT:
                    route_second(n - 1, i)
                if 2 <= n:
                    finish(n - 2, i)

            dve.wait_ge(x2_in[0], 16)
            ffn_step(0)
            ffn_step(1)
            reciprocals(1)
            ffn_step(2)
            ffn_step(3)
            for c in range(1, NCH):
                dve.wait_ge(x2_in[c], 16)
                with dve.Fori(0, QT // 2) as i:
                    chain.enter(i, 2 * LINKS_PER_TILE)
                    for s in range(2):
                        ffn_step(QT * c + s, i)
                    chain.leave(QT // 2)
            ffn_step(NT)
            ffn_step(NT + 1)

        @block.gpsimd
        def _(pool):
            for c in range(NCH):
                for m in range(4):
                    n = 4 * c + m
                    pool.wait_ge(q_split, n + 1)
                    if n:
                        pool.wait_ge(q_stored, 16 * n)
                    pool.dma_start(q_dram[c, :, P * m:P * (m + 1)].rearrange("a r q -> r a q"),
                                   qpart[:, n % 4]).then_inc(q_stored, 16)

            def plain_next():
                pool.nop(nofuse=True)

            def split_max(u, i):
                pool.wait_ge(slot_free, at_loop(NSL * (u // 2) + TURN[u % 2] + 1, i, 2 * NSL))
                if u >= 2:
                    pool.wait_ge(m_stored, at_loop(16 * (u - 1), i, 64))
                plain_next()
                k = 4 * u
                mt, mp = m_t[:, u % 2], m_part[:, u % 2]
                nc.gpsimd.tensor_copy(mp[:, 0], mt).then_inc(pool_chain, 1)
                pool.wait_ge(pool_chain, at_loop(k + 1, i, 16))
                nc.gpsimd.tensor_tensor(out=m_rest[:], in0=mt, in1=mp[:, 0], op=ALU.subtract).then_inc(pool_chain, 1)
                pool.wait_ge(pool_chain, at_loop(k + 2, i, 16))
                plain_next()
                nc.gpsimd.tensor_copy(mp[:, 1], m_rest[:]).then_inc(pool_chain, 1)
                pool.wait_ge(pool_chain, at_loop(k + 3, i, 16))
                nc.gpsimd.tensor_tensor(out=m_rest[:], in0=m_rest[:], in1=mp[:, 1], op=ALU.subtract).then_inc(pool_chain, 1)
                pool.wait_ge(pool_chain, at_loop(k + 4, i, 16))
                plain_next()
                nc.gpsimd.tensor_copy(mp[:, 2], m_rest[:]).then_inc(m_split, 1)

            def zero_future(m, late, i):
                for n, (l, t, off) in enumerate(TILES):
                    if l != late or t < QT * late:
                        continue
                    pool.wait_ge(exp_done, at_loop(NSC * m + SC0[n + 1], i, 2 * NSC))
                    plain_next()
                    d = probs[:, n % 4, :, 0:P]
                    nc.gpsimd.affine_select(out=d, in_=d, compare_op=ALU.is_ge, fill=0.0, base=0,
                                            pattern=[[0, UH], [1, P]], channel_multiplier=-1).then_inc(diag_done, 1)

            def step(k, i=None):
                for late in range(2):
                    if k:
                        zero_future(k - 1, late, i)
                    if k < NK:
                        split_max(2 * k + late, i)

            for b in range(B):
                step(NB * b)
                step(NB * b + 1)
                with pool.Fori(0, PAIRS - 1) as i:
                    step(NB * b + 2, i)
                    step(NB * b + 3, i)
            step(NK)

            def normalise(n, i):
                c = n // QT
                if n >= 2:
                    pool.wait_ge(y_full, at_loop(n - 1, i, 2))
                tok = bass.ds(at_loop((n % QT) * P, i, 2 * P), P)
                nc.gpsimd.tensor_tensor(out=att[:, n % 2], in0=heads_of(c)[:, :, tok], in1=rcps_of(c)[:, :, tok],
                                        op=ALU.mult).then_inc(att_ready, 1)

            def add_bias(n, i):
                pool.wait_ge(x1_ready, at_loop(n + 1, i, 2))
                if n >= 2:
                    pool.wait_ge(y_ready, at_loop(n - 1, i, 2))
                nc.gpsimd.tensor_tensor(out=x1b[:, n % 2], in0=x1[:, n % 2], in1=bias_sb[:], op=ALU.add).then_inc(x1b_ready, 1)

            def ffn_step(n, i=None):
                if n < NT:
                    normalise(n, i)
                if n:
                    add_bias(n - 1, i)

            pool.wait_ge(w2_in, 16 * N_W2)
            pool.wait_ge(heads_in[0], 16 * 4 * UH)
            for n in range(QT):
                ffn_step(n)
            for c in range(1, NCH):
                pool.wait_ge(heads_in[c], 16 * 4 * UH)
                with pool.Fori(0, QT // 2) as i:
                    for s in range(2):
                        ffn_step(QT * c + s, i)
            ffn_step(NT)


def constants():
    import numpy as np

    bf16 = np.dtype("bfloat16")

    def parts(a, n):
        out, rest = [], np.asarray(a, np.float64)
        for _ in range(n):
            out.append(rest.astype(np.float32).astype(bf16))
            rest = rest - out[-1].astype(np.float64)
        return out

    slopes = ((2.0 ** (-(2.0 ** (3 - np.log2(H))))) ** np.arange(1, H + 1)).astype(np.float32).astype(np.float64)
    pos = np.arange(S, dtype=np.float64)
    slope_rows = [np.broadcast_to(a[:, None], (H, S)) for a in parts(slopes, 3)]
    q_rows = np.stack(slope_rows + slope_rows + parts(-slopes[:, None] * pos[None, :], 4))
    q_rows = q_rows.reshape(N_ALIBI, PAIRS, UH, 2, 2, CH).transpose(0, 4, 1, 3, 2, 5).reshape(N_ALIBI, 2 * H * CH)
    one = np.ones(S)
    stairs = [DH * r for r in range(1, N_STAIR + 1)]
    k_rows = np.stack([pos % P] * 3 + [pos - pos % P] * 3 + [one] * 7 + [pos % P >= r for r in stairs]).astype(bf16)
    kmask = np.zeros((P, 3), np.float32)
    for n, (_, b) in enumerate(PARTS):
        kmask[DH * n:DH * (n + 1), b] = 1.0
    return {
        "ident": np.eye(P, dtype=np.float32),
        "identb": np.eye(P, dtype=np.float32).astype(bf16),
        "mneg": (np.triu(np.ones((P, P)), 1) * -1e30).astype(bf16),
        "kmask": kmask,
        "kalibi": k_rows,
        "qalibi": q_rows,
        "stair": np.tile([np.where(pos[:P] < r, -1e30, 0.0) for r in stairs], (1, H * QT)).astype(bf16),
        "iota": np.broadcast_to(np.arange(E, dtype=np.float32), (P, E)).copy(),
    }


def kernel(L0_attn_hidden_states, L0_attn_Wqkv, L0_attn_Wo, L0_ffn_W_base, L0_ffn_b_base, L0_ffn_W_gate, L0_ffn_A, L0_ffn_B):
    import numpy as np
    import concourse.bacc as bacc
    from concourse.bass_utils import run_bass_kernel_spmd as run

    w = np.asarray(L0_attn_Wqkv)
    w_q = w[:, :D].reshape(D, PAIRS, UH, 2, DH).swapaxes(2, 3).reshape(D, D)
    arrays = {
        "x": np.asarray(L0_attn_hidden_states).reshape(B * S, D),
        "wqkv": np.concatenate([w_q] + [w[:, D:D + DH]] * len(PARTS) + [w[:, D + DH:]], axis=1),
        "wo": np.asarray(L0_attn_Wo),
        "wb": np.asarray(L0_ffn_W_base).T,
        "ag": np.concatenate([np.asarray(L0_ffn_A).reshape(E * R, D).T, np.asarray(L0_ffn_W_gate).T], axis=1),
        "lora": np.asarray(L0_ffn_B).transpose(0, 2, 1).reshape(E * R, D),
        "bias": np.broadcast_to(np.asarray(L0_ffn_b_base), (P, D)),
        **constants(),
    }
    nc = bacc.Bacc("TRN2", target_bir_lowering=False, num_devices=1)
    args, fed = [], {}
    for name, a in arrays.items():
        a = np.ascontiguousarray(a)
        fed[f"in_{name}"] = a
        args.append(nc.dram_tensor(f"in_{name}", a.shape, mybir.dt.from_np(a.dtype), kind="ExternalInput").ap())
    out = nc.dram_tensor("out", (B * S, D), F32, kind="ExternalOutput").ap()
    build(nc, *args, out)
    r = run(nc, [fed], core_ids=[0])
    return r.results[0]["out"].reshape(B, S, D)
```

```python
from contextlib import ExitStack

import concourse.bass as bass
from concourse import mybir

F32 = mybir.dt.float32
BF16 = mybir.dt.bfloat16
U32 = mybir.dt.uint32
ALU = mybir.AluOpType
ACT = mybir.ActivationFunctionType
AX_X = mybir.AxisListType.X

P = 128
B, S, D = 2, 1024, 512
H, DH = 32, 16
E, R = 8, 16
KC = D // P
CH = 512
QT = CH // P
NCH = B * S // CH
UH = 4
PAIRS = H // UH // 2
NB = 2 * PAIRS
NK = B * NB
NU = 2 * NK
PARTS = ((0, 0), (0, 1), (0, 2), (1, 0), (1, 1), (2, 0))
ROW_ALIBI = len(PARTS) * DH
N_ALIBI = 10
ROW_MAX = ROW_ALIBI + N_ALIBI
ROWS = ROW_MAX + 3
N_STAIR = P // DH - 1
STAIR_ROWS = ROWS + N_STAIR
QSCALE = DH ** -0.5
EPS = 1e-5
VW = 32
TURN_AFTER = 3
LAG = 2
XW = E * R + E
NT = B * S // P
LINKS_PER_TILE = 16


class Chain:

    def __init__(self, eng, sem):
        self.eng, self.sem, self.n, self.i, self.per = eng, sem, 0, None, 0

    def link(self, ins, plain_next=False):
        ins.then_inc(self.sem, 1)
        self.n += 1
        self.eng.wait_ge(self.sem, self.n if self.i is None else self.n + self.i * self.per)
        if plain_next:
            self.eng.nop(nofuse=True)

    def enter(self, i, per):
        self.i, self.per, self.first = i, per, self.n

    def leave(self, times):
        assert self.n - self.first == self.per
        self.n, self.i = self.first + times * self.per, None


def max_slots(late):
    out = []
    for t in range(QT):
        if late:
            out += [("full", late, t, (j,)) for j in range(UH)]
        per = 2 if t < 2 else 1
        out += [("diag", late, t, tuple(range(j, j + per))) for j in range(0, UH, per)]
    return out


EARLY_SLOTS = len(max_slots(0))
SLOTS = max_slots(0) + max_slots(1)
TURN = [EARLY_SLOTS + TURN_AFTER, len(SLOTS) + 1]
SLOTS.insert(TURN[0], ("turn", 0, None, None))
SLOTS.insert(TURN[1], ("turn", 1, None, None))
NSL = len(SLOTS)
NSB = 3
TILES = [(0, t, P * t) for t in range(QT)] + [(1, t, max(0, P * (t - QT))) for t in range(2 * QT)]
NTI = len(TILES)
DIAGS = 2 * QT
HALVES = [2 if CH - off > 256 else 1 for _, _, off in TILES]
SC0 = [sum(HALVES[:n]) for n in range(NTI + 1)]
NSC = SC0[NTI]


def pe_order(k):
    work = []
    for n, (late, t, off) in enumerate(TILES):
        w = CH - off
        if 1 <= k <= NK:
            work.append((UH // HALVES[n] * w, ("scores", k - 1, (n, 0))))
        m, v = (k - 1, n - LAG) if n >= LAG else (k - 2, n - LAG + NTI)
        if 0 <= m < NK:
            work.append((UH * (CH - TILES[v][2]), ("values", m, v)))
        if 1 <= k <= NK and HALVES[n] == 2:
            work.append((UH // 2 * w, ("scores", k - 1, (n, 1))))
        if k == NK + 1 and n == LAG - 1:
            break
    slots = [("slot", k, r) for r in range(NSL)] if k < NK else []
    total = sum(w for w, _ in work)
    out, done, put = [], 0, 0
    for w, piece in work:
        done += w
        upto = min(NSL - 1, round(NSL * done / (SLOTS_BY * total)))
        out += slots[put:upto]
        put = max(put, upto)
        out.append(piece)
    return out + slots[put:]


OUT_AMONG = [(0, 0), (1, 0), (2, 0), (3, 0), (9, 0), (9, 1), (10, 0), (11, 0)]
TURN_AT = 8


def early_slots():
    out, r = {}, 0
    for (c, m), n in EARLY_COUNTS.items():
        out[c, m] = range(r, r + n)
        r += n
    assert r == NSL
    return out


EARLY_COUNTS = {(2, 0): 4, (2, 1): 4, (2, 2): 4, (2, 3): 6, (2, 4): 6, (3, 0): 5, (3, 1): 4, (3, 2): 4, (3, 3): 4, (3, 4): 1}
RING = [(c, m) if m != "v" else (c - 1, 5) for c in range(NCH) for m in ([0, "v", 1, 2, 3, 4] if c else range(5))] + [(NCH - 1, 5)]
SLOTS_BY = 0.92
assert NSC % 2 == 0 and NSL % NSB == 0 and NTI % 4 == 0


def build(nc, x, wqkv, wo, wb, ag, lora, bias, ident_in, future_in, kmask_in, kalibi_in, qalibi_in, stair_in, iota_in, out):
    with ExitStack() as ctx:
        def sb(name, shape, dt=F32):
            return ctx.enter_context(nc.sbuf_tensor(name, shape, dt))

        def sem(name):
            return ctx.enter_context(nc.semaphore(name))

        q_dram = nc.dram_tensor("q_dram", (NCH, 3, D, CH), BF16, kind="Internal").ap()
        m_dram = nc.dram_tensor("m_dram", (NU, 3, UH * QT, P), BF16, kind="Internal").ap()
        o_dram = nc.dram_tensor("o_dram", (NU, P, CH), F32, kind="Internal").ap()
        sum_dram = nc.dram_tensor("sum_dram", (NU, UH, CH), F32, kind="Internal").ap()
        rcp_dram = nc.dram_tensor("rcp_dram", (NU, UH, CH), F32, kind="Internal").ap()

        AR = PAIRS * CH
        arena = sb("arena", [P, 2 * AR * 2 + H * CH])
        q_op = arena[:, 4 * AR:4 * AR + H * CH].bitcast(BF16)
        q_op_pairs = q_op[:, :].rearrange("p (l g n) -> p l g n", g=PAIRS, l=2)

        def heads_of(c):
            return arena[:, c * 2 * AR:c * 2 * AR + AR].rearrange("p (g q) -> p g q", g=PAIRS)

        def rcps_of(c):
            return arena[:, c * 2 * AR + AR:(c + 1) * 2 * AR].rearrange("p (g q) -> p g q", g=PAIRS)

        work = sb("work", [P, 4 * UH * CH])
        probs = work[:, :].rearrange("p (r j q) -> p r j q", r=4, j=UH)
        xnT = work[:, 0:2 * KC * CH].rearrange("p (r k q) -> p r k q", r=2, k=KC)
        q4 = work[:, 4096:4096 + 2 * CH].rearrange("p (r q) -> p r q", r=2)
        qpart = work[:, 5120:5120 + 6 * CH].bitcast(BF16).rearrange("p (r a q) -> p r a q", r=4, a=3)
        k_tmp = sb("k_tmp", [P, 3 * CH + 3 * CH // 2])

        def x2_of(c):
            at = k_tmp[:, 0:QT * D] if c == 0 else work[:, (c - 1) * QT * D:c * QT * D]
            return at.rearrange("p (n d) -> p n d", d=D)

        x_sb = sb("x_sb", [P, 2, QT, D])
        k_op = sb("k_op", [P, B, S], BF16)
        v_op = sb("v_op", [P, B * S // P, 2, VW])
        wqkv_sb = sb("wqkv_sb", [P, KC, D + 112])
        wo_sb = sb("wo_sb", [P, KC, D])
        wb_sb = sb("wb_sb", [P, KC, D])
        ag_sb = sb("ag_sb", [P, KC, XW])
        lora_sb = sb("lora_sb", [P, D])
        bias_sb = sb("bias_sb", [P, D])
        ident = sb("ident", [P, P])
        future = sb("future", [P, CH])
        kmask = sb("kmask", [P, 3])
        iota = sb("iota", [P, E])
        kv = k_tmp[0:112, 0:CH]
        k_rest = k_tmp[0:96, CH:2 * CH]
        k_sum = k_tmp[0:96, 2 * CH:3 * CH]
        k_part = k_tmp[0:96, 3 * CH:3 * CH + 3 * CH // 2].bitcast(BF16).rearrange("p (a q) -> p a q", a=3)
        stats = sb("stats", [P, QT, 6])
        mv = sb("mv", [P, QT, 2])
        ve = sb("ve", [P, QT])
        lnv = sb("lnv", [P, QT])
        rstd = sb("rstd", [P, QT])
        newt = sb("newt", [P, QT])
        negm = sb("negm", [P, 2, 2, UH * QT])
        m_t = sb("m_t", [UH * QT, 2, P])
        m_rest = sb("m_rest", [UH * QT, P])
        m_part = sb("m_part", [UH * QT, 2, 3, P], BF16)
        o_sb = sb("o_sb", [P, 2, CH])
        sums = sb("sums", [P, 2 * P])
        x1, x1b, xn2 = x_sb[:, 0, 0:2], x_sb[:, 0, 2:4], x_sb[:, 1, 0:2]
        xn2T = x_sb[:, 1, 2:4].rearrange("p r (k q) -> p r k q", k=KC)
        old_w = wqkv_sb[:, :, :].rearrange("p k n -> p (k n)")
        att = old_w[:, 0:2 * D].rearrange("p (r g q) -> p r g q", r=2, g=PAIRS)
        y_sb = old_w[:, 2 * D:4 * D].rearrange("p (r d) -> p r d", r=2)
        ff = sb("ff", [P, 2, 64])
        idx8 = sb("idx8", [P, 2, 8], U32)
        hw = sb("hw", [P, 2, E * R])
        hwT = sb("hwT", [P, 2, P])

        psum = ctx.enter_context(nc.psum_tensor("psum", [P, 8, 512], F32))

        ident_in_sem = sem("ident_in_sem")
        w_in = sem("w_in")
        c_in = sem("c_in")
        w2_in = sem("w2_in")
        ones_set = sem("ones_set")
        x0_in = [sem(f"x0_in{t}") for t in range(QT)]
        x_in = [sem("x_in0"), sem("x_in1")]
        var_ready = sem("var_ready")
        ln_done = sem("ln_done")
        rstd_guess = sem("rstd_guess")
        xn_ready = sem("xn_ready")
        turned = sem("turned")
        xnT_ready = sem("xnT_ready")
        proj_full = sem("proj_full")
        proj_free = sem("proj_free")
        q_hi_ready = sem("q_hi_ready")
        q_split = sem("q_split")
        q_stored = sem("q_stored")
        vt_full = sem("vt_full")
        v_ready = sem("v_ready")
        k_ready = sem("k_ready")
        dve_chain = sem("dve_chain")
        q_loaded = sem("q_loaded")
        slot_full = sem("slot_full")
        slot_free = sem("slot_free")
        max_late = sem("max_late")
        pool_chain = sem("pool_chain")
        m_split = sem("m_split")
        m_stored = sem("m_stored")
        m_loaded = sem("m_loaded")
        s_full = sem("s_full")
        exp_done = sem("exp_done")
        diag_done = sem("diag_done")
        pv_done = sem("pv_done")
        o_copied = sem("o_copied")
        o_stored = sem("o_stored")
        sums_in = sem("sums_in")
        rcp_ready = sem("rcp_ready")
        rcp_stored = sem("rcp_stored")
        heads_in = [sem(f"heads_in{c}") for c in range(NCH)]
        x2_in = [sem(f"x2_in{c}") for c in range(NCH)]
        att_ready = sem("att_ready")
        y_full = sem("y_full")
        x1_ready = sem("x1_ready")
        var2_ready = sem("var2_ready")
        ln2_done = sem("ln2_done")
        guess2 = sem("guess2")
        xn2_ready = sem("xn2_ready")
        x1b_ready = sem("x1b_ready")
        turned2 = sem("turned2")
        xn2T_ready = sem("xn2T_ready")
        h_full = sem("h_full")
        gap_ready = sem("gap_ready")
        e2_ready = sem("e2_ready")
        hw_ready = sem("hw_ready")
        hw_turned = sem("hw_turned")
        hwT_ready = sem("hwT_ready")
        z_full = sem("z_full")
        y_ready = sem("y_ready")
        out_sem = [sem("out_sem0"), sem("out_sem1")]

        block = ctx.enter_context(nc.Block())
        x_rows = x.rearrange("(c t p) d -> c p t d", t=QT, p=P)
        out_rows = out.rearrange("(n p) d -> n p d", p=P)
        N_W, N_C, N_W2 = 5, 7, 5

        def at_loop(base, i, per):
            return base if i is None else base + i * per

        def unit_col(u, j, i):
            g, s = (u % (2 * NB)) // 4, (u // 2) % 2
            return at_loop((((PAIRS * (u % 2) + g) * 2 + s) * UH + j) * CH, i, 2 * UH * CH)

        @block.sync
        def _(sp):
            for t in range(QT):
                sp.dma_start(x_sb[:, 0, t], x_rows[0][:, t]).then_inc(x0_in[t], 16)
            for k in range(KC):
                sp.dma_start(wqkv_sb[:, k], wqkv[P * k:P * (k + 1)]).then_inc(w_in, 16)
            sp.dma_start(x_sb[:, 1], x_rows[1]).then_inc(x_in[1], 16)
            sp.dma_start(future[:], future_in).then_inc(c_in, 16)
            for b in range(B):
                sp.dma_start(k_op[ROW_ALIBI:STAIR_ROWS, b, :], kalibi_in).then_inc(c_in, 16)
            sp.dma_start(q_op[ROW_ALIBI:ROW_MAX, :], qalibi_in).then_inc(c_in, 16)
            for a in range(2):
                sp.dma_start(q_op[ROWS:STAIR_ROWS, a * H * CH:(a + 1) * H * CH], stair_in).then_inc(c_in, 16)
            sp.dma_start(iota[:], iota_in).then_inc(c_in, 16)
            for c in (2, 3):
                sp.wait_ge(turned, QT * (c - 1))
                sp.dma_start(x_sb[:, c % 2], x_rows[c]).then_inc(x_in[c % 2], 16)

            def load_queries(c):
                sp.wait_ge(q_loaded, 16 * 6 * c)
                sp.wait_ge(q_stored, 16 * 4 * (c + 1))
                for n, (a, _) in enumerate(PARTS):
                    sp.dma_start(q_op_pairs[DH * n:DH * (n + 1), c % 2].rearrange("d g (h q) -> d (g h) q", q=CH),
                                 q_dram[c, a].rearrange("(h d) q -> d h q", d=DH)).then_inc(q_loaded, 16)

            def load_pair(g, i=None):
                sp.wait_ge(q_loaded, at_loop(16 * 12 * (1 + g), i, 16 * 12))
                plain_next()
                sp.wait_ge(s_full, at_loop(NSC * 2 * (g + 1), i, 2 * NSC))
                plain_next()
                gi = at_loop(g, i, 1)
                for late in range(2):
                    for n, (a, _) in enumerate(PARTS):
                        sp.dma_start(q_op_pairs[DH * n:DH * (n + 1), late, bass.ds(gi, 1)].rearrange("d g (h q) -> d (g h) q", q=CH),
                                     q_dram[NCH // 2 + late, a, bass.ds(gi * P, P)].rearrange("(h d) q -> d h q", d=DH)
                                     ).then_inc(q_loaded, 16)

            def plain_next():
                sp.nop(nofuse=True)

            def store_unit(u, i=None):
                uu = at_loop(u, i, 4)
                sp.wait_ge(o_copied, at_loop(u + 1, i, 4))
                plain_next()
                if u:
                    sp.wait_ge(o_stored, at_loop(32 * u, i, 128))
                    plain_next()
                sp.dma_start(o_dram[bass.ds(uu, 1)].rearrange("u p q -> (u p) q"), o_sb[:, u % 2]).then_inc(o_stored, 16)
                ones = DH * (1 - (u // 2) % 2)
                sp.dma_start(sum_dram[bass.ds(uu, 1)].rearrange("u j q -> (u j) q"),
                             o_sb[ones:P:VW, u % 2]).then_inc(o_stored, 16)

            def max_rows(u, i=None):
                uu = at_loop(u, i, 4)
                sp.wait_ge(m_split, at_loop(u + 1, i, 4))
                plain_next()
                sp.dma_start(m_dram[bass.ds(uu, 1)].rearrange("u a n q -> n (u a) q"), m_part[:, u % 2]).then_inc(m_stored, 16)
                sp.wait_ge(m_stored, at_loop(16 * (u + 1), i, 64))
                plain_next()
                if u:
                    sp.wait_ge(m_loaded, at_loop(16 * u, i, 64))
                    plain_next()
                sp.dma_start(q_op[ROW_MAX:ROWS, bass.ds(unit_col(u, 0, i), UH * CH)],
                             m_dram[bass.ds(uu, 1)].rearrange("u a n q -> (u a) (n q)")).then_inc(m_loaded, 16)

            def load_sums(b):
                sp.wait_ge(o_stored, 32 * 2 * NB * (b + 1))
                if b:
                    sp.wait_ge(rcp_stored, 16 * b)
                sp.dma_start(sums[:], sum_dram[2 * NB * b:2 * NB * (b + 1)].rearrange("u j (s q) -> (u j s) q", s=2)
                             ).then_inc(sums_in, 16)

            def store_rcps(b):
                sp.wait_ge(rcp_ready, b + 1)
                sp.dma_start(rcp_dram[2 * NB * b:2 * NB * (b + 1)].rearrange("u j (s q) -> (u j s) q", s=2), sums[:]
                             ).then_inc(rcp_stored, 16)

            def load_heads(c):
                b = c // 2
                sp.wait_ge(rcp_stored, 16 * (b + 1))
                units = slice(2 * NB * b, 2 * NB * (b + 1))
                o_c = o_dram[units].rearrange("(g s l) p q -> l s p g q", s=2, l=2)[c % 2]
                r_c = rcp_dram[units].rearrange("(g s l) j q -> l s j g q", s=2, l=2)[c % 2]
                for j in range(UH):
                    for s in range(2):
                        p0 = VW * j + DH * s
                        sp.dma_start(heads_of(c)[p0:p0 + DH], o_c[s, p0:p0 + DH]).then_inc(heads_in[c], 16)
                        sp.dma_start(rcps_of(c)[p0:p0 + DH],
                                     r_c[s, j:j + 1].broadcast_to((DH, PAIRS, CH))).then_inc(heads_in[c], 16)

            def step(k, i=None):
                if k >= 2:
                    store_unit(2 * k - 3, i)
                if k < NK:
                    max_rows(2 * k, i)
                if 1 <= k <= NK:
                    store_unit(2 * k - 2, i)
                if k < NK:
                    max_rows(2 * k + 1, i)

            load_queries(0)
            load_queries(1)
            sp.dma_start(wo_sb[:], wo.rearrange("(k p) n -> p k n", p=P)).then_inc(w2_in, 16)
            sp.dma_start(wb_sb[:], wb.rearrange("(k p) n -> p k n", p=P)).then_inc(w2_in, 16)
            sp.dma_start(ag_sb[:], ag.rearrange("(k p) n -> p k n", p=P)).then_inc(w2_in, 16)
            sp.dma_start(lora_sb[:], lora).then_inc(w2_in, 16)
            sp.dma_start(bias_sb[:], bias).then_inc(w2_in, 16)
            step(0)
            sp.wait_ge(k_ready, NCH)
            sp.wait_ge(v_ready, NCH)
            sp.dma_start(x2_of(0), x_rows[0]).then_inc(x2_in[0], 16)
            step(1)
            with sp.Fori(0, PAIRS - 1) as i:
                step(2, i)
                load_pair(0, i)
                step(3, i)
            step(NB)
            load_pair(PAIRS - 1)
            step(NB + 1)
            load_sums(0)
            step(NB + 2)
            store_rcps(0)
            load_heads(0)
            step(NB + 3)
            load_heads(1)
            with sp.Fori(0, PAIRS - 2) as i:
                step(NB + 4, i)
                step(NB + 5, i)
            step(NK)
            step(NK + 1)
            sp.wait_ge(pv_done, NTI * NK)
            load_sums(1)
            sp.dma_start(x2_of(1), x_rows[1]).then_inc(x2_in[1], 16)
            store_rcps(1)
            for c in (2, 3):
                load_heads(c)
                sp.dma_start(x2_of(c), x_rows[c]).then_inc(x2_in[c], 16)
            with sp.Fori(0, NT // 2) as i:
                for s in range(2):
                    sp.wait_ge(y_ready, i * 2 + s + 1)
                    plain_next()
                    sp.dma_start(out_rows[bass.ds(i * 2 + s, 1)].rearrange("n p d -> (n p) d"), y_sb[:, s]).then_inc(out_sem[s], 16)
            for s in range(2):
                sp.wait_ge(out_sem[s], 16 * (NT // 2))

        @block.tensor
        def _(pe):
            def transposes(c, tiles=range(QT)):
                for t in tiles:
                    n = QT * c + t
                    pe.wait_ge(xn_ready, n + 1)
                    if n >= 2:
                        pe.wait_ge(xnT_ready, n - 1)
                    for k in range(KC):
                        last = nc.tensor.transpose(psum[:, NSB + n % 2, k * P:(k + 1) * P],
                                                   x_sb[:, c % 2, t, k * P:(k + 1) * P], ident[:])
                    last.then_inc(turned, 1)

            def ring_bank(c, m):
                n = RING.index((c, m))
                if n >= 3:
                    old_c, old_m = RING[n - 3]
                    if old_m < 5:
                        pe.wait_ge(proj_free, 5 * old_c + old_m + 1)
                    else:
                        pe.wait_ge(v_ready, old_c + 1)
                return psum[:, 5 + n % 3]

            def project(c, m, slots):
                if m == 0:
                    pe.wait_ge(xnT_ready, QT * (c + 1))
                width = P if m < 4 else 112
                bank = ring_bank(c, m)
                for k in range(KC):
                    last = nc.tensor.matmul(bank[0:width], wqkv_sb[:, k, P * m:P * m + width], xnT[:, c % 2, k, :],
                                            start=(k == 0), stop=(k == KC - 1))
                    if k == KC - 1:
                        last.then_inc(proj_full, 1)
                    for r in slots[len(slots) * k // KC:len(slots) * (k + 1) // KC]:
                        max_slot(0, r, None)

            def values(c):
                bank = ring_bank(c, 5)
                pe.wait_ge(proj_free, 5 * c + 5)
                for t in range(QT):
                    last = nc.tensor.transpose(bank[:, 112 * t:112 * (t + 1)], kv[:, t * P:(t + 1) * P], ident[0:112, 0:112])
                last.then_inc(vt_full, 1)

            def max_slot(k, r, i):
                kind, late, t, js = SLOTS[r]
                idx, per = NSL * k + r, 2 * NSL
                if idx >= NSB:
                    pe.wait_ge(slot_free, at_loop(idx - NSB + 1, i, per))
                bank = psum[:, idx % NSB]
                if kind == "turn":
                    if late:
                        pe.wait_ge(max_late, at_loop(k + 1, i, 2))
                    else:
                        pe.wait_ge(slot_free, at_loop(NSL * k + EARLY_SLOTS, i, per))
                    nc.tensor.transpose(bank[0:UH * QT, 0:P], negm[:, late, 0, :], ident[:]).then_inc(slot_full, 1)
                    return
                if k == 0 and r == EARLY_SLOTS:
                    pe.wait_ge(k_ready, 2)
                    pe.wait_ge(q_loaded, 16 * 6 * 2)
                b = k // NB
                width = P * (t + 1) if kind == "diag" else CH
                k0 = CH * late if kind == "diag" else 0
                for a, j in enumerate(js):
                    col = unit_col(2 * k + late, j, i) + t * P
                    last = nc.tensor.matmul(bank[:, a * width:(a + 1) * width], q_op[0:ROW_MAX, bass.ds(col, P)],
                                            k_op[0:ROW_MAX, b, k0:k0 + width],
                                            start=True, stop=True)
                last.then_inc(slot_full, 1)

            def scores(m, at, i):
                n, hp = at
                late, t, off = TILES[n]
                b, w = m // NB, CH - off
                if t == 0 and hp == 0:
                    pe.wait_ge(m_loaded, at_loop(16 * (2 * m + late + 1), i, 64))
                heads = UH // HALVES[n]
                idx = NSC * m + SC0[n] + hp
                if idx >= 2:
                    pe.wait_ge(exp_done, at_loop(idx - 1, i, 2 * NSC))
                for a in range(heads):
                    col = unit_col(2 * m + late, heads * hp + a, i) + off
                    at = psum[:, NSB + 2 * (idx % 2) + (a if heads == 2 else a * w // CH)]
                    at = at[:, 0:w] if heads == 2 else at[:, a * w % CH:a * w % CH + w]
                    diag = P if t >= QT * late else 0
                    if diag:
                        last = nc.tensor.matmul(at[:, 0:P], k_op[0:STAIR_ROWS, b, t * P:(t + 1) * P],
                                                q_op[0:STAIR_ROWS, bass.ds(col, P)], start=True, stop=True)
                    if diag < w:
                        last = nc.tensor.matmul(at[:, diag:w], k_op[0:ROWS, b, t * P:(t + 1) * P],
                                                q_op[0:ROWS, bass.ds(col + diag, w - diag)], start=True, stop=True)
                last.then_inc(s_full, 1)

            def values_product(m, n, i):
                late, t, off = TILES[n]
                b, u = m // NB, 2 * m + late
                if t == 0 and not u:
                    pe.wait_ge(v_ready, NCH)
                if t == 0 and u:
                    pe.wait_ge(o_copied, at_loop(u, i, 4))
                pe.wait_ge(exp_done, at_loop(NSC * m + SC0[n + 1], i, 2 * NSC))
                if t >= QT * late:
                    pe.wait_ge(diag_done, at_loop(DIAGS * m + QT * late + t - QT * late + 1, i, 2 * DIAGS))
                last_tile = QT * (1 + late) - 1
                for j in range(UH):
                    last = nc.tensor.matmul(psum[VW * j:VW * (j + 1), 7, off:CH], v_op[:, b * (S // P) + t, m % 2, :],
                                            probs[:, n % 4, j, 0:CH - off], start=(t == 0), stop=(t == last_tile))
                last.then_inc(pv_done, 1)

            def step(k, i=None):
                for what, m, n in pe_order(k):
                    if k == 1 and what == "scores" and n == (0, 1):
                        values(NCH - 1)
                    if k == NK and what == "scores" and n in OUT_AMONG:
                        tile, g = divmod(OUT_AMONG.index(n), PAIRS)
                        out_proj(tile, None, (g,))
                    if k == NK and what == "scores" and n == (TURN_AT, 0):
                        turn_xn2(0, None)
                    {"slot": max_slot, "scores": scores, "values": values_product}[what](m, n, i)

            def out_proj(n, i, some=range(PAIRS)):
                if n == 0 and 0 in some:
                    pe.wait_ge(slot_free, NSL * NK)
                pe.wait_ge(att_ready, at_loop(n + 1, i, 2))
                if n >= 2:
                    pe.wait_ge(x1_ready, at_loop(n - 1, i, 2))
                for g in some:
                    last = nc.tensor.matmul(psum[:, n % 2], att[:, n % 2, g, :], wo_sb[:, g, :], start=(g == 0), stop=(g == PAIRS - 1))
                if g == PAIRS - 1:
                    last.then_inc(y_full, 1)

            def turn_xn2(n, i):
                pe.wait_ge(xn2_ready, at_loop(n + 1, i, 2))
                if n >= 2:
                    pe.wait_ge(xn2T_ready, at_loop(n - 1, i, 2))
                for k in range(KC):
                    last = nc.tensor.transpose(psum[:, 2 + n % 2, k * P:(k + 1) * P], xn2[:, n % 2, k * P:(k + 1) * P], ident[:])
                last.then_inc(turned2, 1)

            def base_and_lora_in(n, i):
                pe.wait_ge(xn2T_ready, at_loop(n + 1, i, 2))
                if n >= 1:
                    pe.wait_ge(hw_ready, at_loop(n, i, 2))
                for k in range(KC):
                    last = nc.tensor.matmul(psum[:, 4, 0:XW], xn2T[:, n % 2, k, :], ag_sb[:, k, :], start=(k == 0), stop=(k == KC - 1))
                last.then_inc(h_full, 1)
                if n >= 2:
                    pe.wait_ge(y_ready, at_loop(n - 1, i, 2))
                for k in range(KC):
                    nc.tensor.matmul(psum[:, 6 + n % 2], xn2T[:, n % 2, k, :], wb_sb[:, k, :], start=(k == 0), stop=False)

            def turn_hw(n, i):
                pe.wait_ge(hw_ready, at_loop(n + 1, i, 2))
                if n >= 1:
                    pe.wait_ge(hwT_ready, at_loop(n, i, 2))
                nc.tensor.transpose(psum[:, 5, 0:P], hw[:, n % 2], ident[:]).then_inc(hw_turned, 1)

            def lora_out(n, i):
                pe.wait_ge(hwT_ready, at_loop(n + 1, i, 2))
                nc.tensor.matmul(psum[:, 6 + n % 2], hwT[:, n % 2], lora_sb[:], start=False, stop=True).then_inc(z_full, 1)

            def ffn_step(n, i=None):
                if 2 <= n <= NT:
                    turn_xn2(n - 1, i)
                if 2 <= n < NT:
                    out_proj(n, i)
                if 2 <= n:
                    turn_hw(n - 2, i)
                if 1 <= n <= NT:
                    base_and_lora_in(n - 1, i)
                if 2 <= n:
                    lora_out(n - 2, i)

            pe.wait_ge(ident_in_sem, 16)
            transposes(0)
            pe.wait_ge(w_in, 16 * N_W)
            among = early_slots()
            for c in range(NCH):
                if c == 2:
                    pe.wait_ge(c_in, 16 * N_C)
                    pe.wait_ge(k_ready, 1)
                    pe.wait_ge(q_loaded, 16 * 6)
                for m in range(5):
                    project(c, m, among.get((c, m), ()))
                    if m == 0 and c:
                        values(c - 1)
                    if m in (1, 2) and c + 1 < NCH:
                        transposes(c + 1, (2 * m - 2, 2 * m - 1))
            for b in range(B):
                if b:
                    pe.wait_ge(k_ready, NCH)
                    pe.wait_ge(q_loaded, 16 * 6 * 2 * PAIRS)
                    step(NB * b)
                step(NB * b + 1)
                if b:
                    pe.wait_ge(q_loaded, 16 * 6 * 2 * (1 + PAIRS))
                with pe.Fori(0, PAIRS - 1) as i:
                    step(NB * b + 2, i)
                    step(NB * b + 3, i)
            pe.wait_ge(w2_in, 16 * N_W2)
            step(NK)
            step(NK + 1)

            for n in range(QT):
                ffn_step(n)
            for c in range(1, NCH):
                with pe.Fori(0, QT // 2) as i:
                    for s in range(2):
                        ffn_step(QT * c + s, i)
            ffn_step(NT)
            ffn_step(NT + 1)

        @block.scalar
        def _(act):
            def rstd_first(c):
                act.wait_ge(var_ready, c + 1)
                nc.scalar.activation(lnv[:], ve[:], ACT.Ln).then_inc(ln_done, 1)
                act.wait_ge(ln_done, c + 1)
                nc.scalar.activation(rstd[:], lnv[:], ACT.Exp, scale=-0.5).then_inc(rstd_guess, 1)

            def xnT_copies(c, tiles=range(QT)):
                for t in tiles:
                    n = QT * c + t
                    act.wait_ge(turned, n + 1)
                    if t == 0 and c >= 2:
                        act.wait_ge(proj_full, 5 * (c - 1))
                    nc.scalar.copy(xnT[:, c % 2, :, t * P:(t + 1) * P],
                                   psum[:, NSB + n % 2].rearrange("p (k q) -> p k q", k=KC)).then_inc(xnT_ready, 1)

            def query_hi(c, m):
                n = 4 * c + m
                act.wait_ge(proj_full, 5 * c + m + 1)
                if n >= 2:
                    act.wait_ge(q_split, n - 1)
                if n >= 4:
                    act.wait_ge(q_stored, 16 * (n - 3))
                nc.scalar.mul(q4[:, n % 2], psum[:, 5 + RING.index((c, m)) % 3], QSCALE).then_inc(proj_free, 1)
                act.wait_ge(proj_free, 5 * c + m + 1)
                nc.scalar.copy(qpart[:, n % 4, 0], q4[:, n % 2]).then_inc(q_hi_ready, 1)

            def keys_values(c):
                act.wait_ge(proj_full, 5 * c + 5)
                if c:
                    act.wait_ge(k_ready, c)
                    act.wait_ge(vt_full, c)
                nc.scalar.copy(kv[:], psum[0:112, 5 + RING.index((c, 4)) % 3]).then_inc(proj_free, 1)

            act.dma_start(ident[:], ident_in).then_inc(ident_in_sem, 16)
            act.dma_start(kmask[:], kmask_in).then_inc(w_in, 16)
            act.preload_act_table_set("natural_log_exp_and_others")
            rstd_first(0)
            xnT_copies(0)
            rstd_first(1)
            for c in range(NCH):
                for m in range(4):
                    query_hi(c, m)
                    if m == 1 and c + 2 < NCH:
                        rstd_first(c + 2)
                    if m in (1, 2) and c + 1 < NCH:
                        xnT_copies(c + 1, (2 * m - 2, 2 * m - 1))
                keys_values(c)

            def exps(m, n, i):
                w = CH - TILES[n][2]
                if NTI * m + n == 2:
                    act.wait_ge(q_stored, 16 * 4 * NCH)
                if NTI * m + n >= 4:
                    act.wait_ge(pv_done, at_loop(NTI * m + n - 3, i, 2 * NTI))
                heads = UH // HALVES[n]
                for hp in range(HALVES[n]):
                    idx = NSC * m + SC0[n] + hp
                    act.wait_ge(s_full, at_loop(idx + 1, i, 2 * NSC))
                    b0 = NSB + 2 * (idx % 2)
                    if heads == 2:
                        src = psum[:, b0:b0 + 2, 0:w]
                    else:
                        src = psum[:, b0:b0 + 2].rearrange("p b q -> p (b q)")[:, 0:UH * w].rearrange("p (j q) -> p j q", j=UH)
                    nc.scalar.activation(probs[:, n % 4, heads * hp:heads * (hp + 1), 0:w], src, ACT.Exp).then_inc(exp_done, 1)
                    if hp == 0 and n == LAG - 1 and m:
                        copy_unit(2 * m - 1, i)
                    if hp == 0 and n == QT + LAG - 1:
                        copy_unit(2 * m, i)

            def copy_unit(u, i=None):
                act.wait_ge(pv_done, at_loop(NTI * (u // 2) + (NTI if u % 2 else QT), i, 2 * NTI))
                if u >= 2:
                    act.wait_ge(o_stored, at_loop(32 * (u - 1), i, 128))
                nc.scalar.copy(o_sb[:, u % 2], psum[:, 7]).then_inc(o_copied, 1)

            def step(k, i=None):
                m = k - 1
                for n in range(NTI):
                    exps(m, n, i)
                    if k == NK and n == 5:
                        guess(0, None)
                    if k == NK and n == TURN_AT:
                        copy_xn2T(0, None)
                    if k == NK and n == NTI - 1:
                        guess(1, None)

            def guess(n, i):
                act.wait_ge(var2_ready, at_loop(n + 1, i, 2))
                nc.scalar.activation(ff[:, n % 2, 2:3], ff[:, n % 2, 1:2], ACT.Ln).then_inc(ln2_done, 1)
                act.wait_ge(ln2_done, at_loop(n + 1, i, 2))
                nc.scalar.activation(ff[:, n % 2, 3:4], ff[:, n % 2, 2:3], ACT.Exp, scale=-0.5).then_inc(guess2, 1)

            def copy_xn2T(n, i):
                act.wait_ge(turned2, at_loop(n + 1, i, 2))
                if n >= 2:
                    act.wait_ge(z_full, at_loop(n - 1, i, 2))
                nc.scalar.copy(xn2T[:, n % 2], psum[:, 2 + n % 2].rearrange("p (k q) -> p k q", k=KC)).then_inc(xn2T_ready, 1)

            def second_weight(n, i):
                act.wait_ge(gap_ready, at_loop(n + 1, i, 2))
                nc.scalar.activation(ff[:, n % 2, 6:7], ff[:, n % 2, 5:6], ACT.Exp).then_inc(e2_ready, 1)

            def copy_hwT(n, i):
                act.wait_ge(hw_turned, at_loop(n + 1, i, 2))
                if n >= 2:
                    act.wait_ge(z_full, at_loop(n - 1, i, 2))
                nc.scalar.copy(hwT[:, n % 2], psum[:, 5, 0:P]).then_inc(hwT_ready, 1)

            def ffn_step(n, i=None):
                if 2 <= n <= NT:
                    copy_xn2T(n - 1, i)
                if 2 <= n:
                    copy_hwT(n - 2, i)
                if 2 <= n < NT:
                    guess(n, i)
                if 1 <= n <= NT:
                    second_weight(n - 1, i)

            step(1)
            for b in range(B):
                if b:
                    step(NB * b)
                    step(NB * b + 1)
                with act.Fori(0, PAIRS - 1) as i:
                    step(NB * b + 2, i)
                    step(NB * b + 3, i)
            step(NK)
            copy_unit(NU - 1)

            for n in range(QT):
                ffn_step(n)
            for c in range(1, NCH):
                with act.Fori(0, QT // 2) as i:
                    for s in range(2):
                        ffn_step(QT * c + s, i)
            ffn_step(NT)
            ffn_step(NT + 1)

        @block.vector
        def _(dve):
            chain = Chain(dve, dve_chain)
            link = chain.link

            nc.vector.memset(v_op[:], 1.0).then_inc(ones_set, 1)

            def newton(r, v, t):
                link(nc.vector.tensor_tensor(t, r, r, ALU.mult))
                link(nc.vector.tensor_tensor(t, t, v, ALU.mult))
                link(nc.vector.tensor_scalar(t, t, -0.5, 1.5, ALU.mult, ALU.add))
                link(nc.vector.tensor_tensor(r, r, t, ALU.mult))

            def statistics(c):
                for t in range(QT):
                    if c == 0:
                        dve.wait_ge(x0_in[t], 16)
                    elif t == 0:
                        dve.wait_ge(x_in[c % 2], 16 * (1 + (c == 3)))
                    last = nc.vector.bn_stats(stats[:, t], x_sb[:, c % 2, t])
                link(last)
                for t in range(QT):
                    last = nc.vector.bn_aggr(mv[:, t], stats[:, t])
                link(last)
                nc.vector.tensor_scalar(ve[:], mv[:, :, 1], EPS, None, ALU.add).then_inc(var_ready, 1)

            def normalised(c, tiles):
                if tiles[0] == 0:
                    dve.wait_ge(rstd_guess, c + 1)
                    dve.wait_ge(var_ready, c + 1)
                    newton(rstd[:], ve[:], newt[:])
                for t in tiles:
                    nc.vector.tensor_scalar(x_sb[:, c % 2, t], x_sb[:, c % 2, t], mv[:, t, 0:1], rstd[:, t:t + 1],
                                            ALU.subtract, ALU.mult).then_inc(xn_ready, 1)

            def split_queries(c, m):
                n = 4 * c + m
                dve.wait_ge(q_hi_ready, n + 1)
                link(nc.vector.tensor_tensor(q4[:, n % 2], q4[:, n % 2], qpart[:, n % 4, 0], ALU.subtract))
                link(nc.vector.tensor_copy(qpart[:, n % 4, 1], q4[:, n % 2]))
                nc.vector.tensor_tensor(qpart[:, n % 4, 2], q4[:, n % 2], qpart[:, n % 4, 1], ALU.subtract).then_inc(q_split, 1)

            def split_keys(c, piece):
                if piece == 0:
                    dve.wait_ge(proj_free, 5 * c + 5)
                    link(nc.vector.tensor_copy(k_part[:, 0], kv[0:96]))
                elif piece == 1:
                    link(nc.vector.tensor_tensor(k_rest[:], kv[0:96], k_part[:, 0], ALU.subtract))
                elif piece == 2:
                    link(nc.vector.tensor_copy(k_part[:, 1], k_rest[:]))
                elif piece == 3:
                    link(nc.vector.tensor_tensor(k_part[:, 2], k_rest[:], k_part[:, 1], ALU.subtract))
                elif piece == 4:
                    link(nc.vector.tensor_scalar(k_sum[:], k_part[:, 0], kmask[0:96, 0:1], None, ALU.mult))
                elif piece == 5:
                    link(nc.vector.scalar_tensor_tensor(k_sum[:], k_part[:, 1], kmask[0:96, 1:2], k_sum[:], ALU.mult, ALU.add))
                else:
                    nc.vector.scalar_tensor_tensor(k_op[0:96, c // 2, (c % 2) * CH:(c % 2 + 1) * CH], k_part[:, 2],
                                                   kmask[0:96, 2:3], k_sum[:], ALU.mult, ALU.add).then_inc(k_ready, 1)

            KEY_PIECES = 7

            def copy_values(c):
                dve.wait_ge(vt_full, c + 1)
                v = psum[:, 5 + RING.index((c, 5)) % 3, 0:QT * 112].rearrange("p (t n) -> p t n", t=QT)[:, :, 96:112]
                nc.vector.tensor_copy(v_op[:, QT * c:QT * (c + 1), 0, 0:DH], v)
                nc.vector.tensor_copy(v_op[:, QT * c:QT * (c + 1), 1, DH:VW], v).then_inc(v_ready, 1)

            def step(k, i=None, some=range(NSL)):
                for r in some:
                    kind, late, t, js = SLOTS[r]
                    idx = NSL * k + r
                    if kind == "turn":
                        u = 2 * k + late
                        if late:
                            dve.wait_ge(slot_free, at_loop(idx, i, 2 * NSL))
                            nc.vector.tensor_tensor(negm[:, 1, 0, :], negm[:, 1, 0, :], negm[:, 1, 1, :], ALU.min
                                                    ).then_inc(max_late, 1)
                        dve.wait_ge(slot_full, at_loop(idx + 1, i, 2 * NSL))
                        if u >= 2:
                            dve.wait_ge(m_split, at_loop(u - 1, i, 4))
                        nc.vector.tensor_copy(m_t[:, u % 2], psum[0:UH * QT, idx % NSB, 0:P]).then_inc(slot_free, 1)
                        continue
                    dve.wait_ge(slot_full, at_loop(idx + 1, i, 2 * NSL))
                    width = P * (t + 1) if kind == "diag" else CH
                    where = 1 if kind == "full" else 0
                    if kind == "diag":
                        if i is not None:
                            dve.nop(nofuse=True)
                        for a, j in enumerate(js):
                            keys = psum[:, idx % NSB, a * width:(a + 1) * width]
                            last = nc.vector.tensor_tensor_reduce(keys, keys, future[:, CH - width:CH], -1.0, 3e38, ALU.add, ALU.min,
                                                                  negm[:, late, 0, j * QT + t:j * QT + t + 1])
                        last.then_inc(slot_free, 1)
                        continue
                    dst = negm[:, late, where, :].rearrange("p (j t) -> p j t", t=QT)[:, js[0]:js[-1] + 1, t]
                    nc.vector.tensor_reduce(dst, psum[:, idx % NSB, 0:len(js) * width].rearrange("p (a k) -> p a k", a=len(js)),
                                            AX_X, ALU.max, negate=True).then_inc(slot_free, 1)

            def reciprocals(b):
                dve.wait_ge(sums_in, 16 * (b + 1))
                nc.vector.reciprocal(sums[:], sums[:]).then_inc(rcp_ready, 1)

            dve.wait_ge(ones_set, 1)
            for c in range(2):
                statistics(c)
                normalised(c, range(QT))
            dve.wait_ge(w_in, 16 * N_W)
            dve.wait_ge(c_in, 16 * N_C)
            among = early_slots()
            for c in range(NCH):
                for m in range(5):
                    for n, r in enumerate(among.get((c, m), ())):
                        step(0, None, (r,))
                        if n < KC and m * KC + n < KEY_PIECES:
                            split_keys(c - 1, m * KC + n)
                    if m == 0 and c:
                        copy_values(c - 1)
                    if m < 4:
                        split_queries(c, m)
                    if c + 2 < NCH and m < 3:
                        if m == 0:
                            statistics(c + 2)
                        else:
                            normalised(c + 2, (0, 1) if m == 1 else (2, 3))
                if c == 0:
                    for piece in range(KEY_PIECES):
                        split_keys(0, piece)
            copy_values(NCH - 1)
            for piece in range(KEY_PIECES):
                step(1, None, range(2 * piece, 2 * piece + 2))
                split_keys(NCH - 1, piece)
            step(1, None, range(2 * KEY_PIECES, NSL))

            for b in range(B):
                if b:
                    step(NB * b)
                    step(NB * b + 1)
                    step(NB * b + 2)
                    reciprocals(0)
                    step(NB * b + 3)
                with dve.Fori(0, PAIRS - 1 - b) as i:
                    step(NB * b + 2 + 2 * b, i)
                    step(NB * b + 3 + 2 * b, i)

            def residual(n, i):
                dve.wait_ge(y_full, at_loop(n + 1, i, 2))
                if n >= 2:
                    dve.wait_ge(x1b_ready, at_loop(n - 1, i, 2))
                nc.vector.tensor_tensor(x1[:, n % 2], x2_of(n // QT)[:, bass.ds(at_loop(n % QT, i, 2), 1)].rearrange("p n d -> p (n d)"), psum[:, n % 2], ALU.add).then_inc(x1_ready, 1)
                dve.wait_ge(x1_ready, at_loop(n + 1, i, 2))
                link(nc.vector.bn_stats(stats[:, n % 2], x1[:, n % 2]), plain_next=True)
                link(nc.vector.bn_aggr(mv[:, n % 2], stats[:, n % 2]))
                nc.vector.tensor_scalar(ff[:, n % 2, 1:2], mv[:, n % 2, 1:2], EPS, None, ALU.add).then_inc(var2_ready, 1)

            def norm2(n, i):
                dve.wait_ge(guess2, at_loop(n + 1, i, 2))
                newton(ff[:, n % 2, 3:4], ff[:, n % 2, 1:2], ff[:, n % 2, 4:5])
                if n >= 2:
                    dve.wait_ge(turned2, at_loop(n - 1, i, 2))
                nc.vector.tensor_scalar(xn2[:, n % 2], x1[:, n % 2], mv[:, n % 2, 0:1], ff[:, n % 2, 3:4],
                                        ALU.subtract, ALU.mult).then_inc(xn2_ready, 1)

            def route_first(n, i):
                f = ff[:, n % 2]
                dve.wait_ge(h_full, at_loop(n + 1, i, 2))
                link(nc.vector.tensor_copy(f[:, 8:16], psum[:, 4, E * R:XW]), plain_next=True)
                link(nc.vector.max(f[:, 16:24], f[:, 8:16]), plain_next=True)
                link(nc.vector.max_index(idx8[:, n % 2], f[:, 16:24], f[:, 8:16]))
                link(nc.vector.tensor_copy(f[:, 24:32], idx8[:, n % 2]))
                nc.vector.tensor_tensor(f[:, 5:6], f[:, 17:18], f[:, 16:17], ALU.subtract).then_inc(gap_ready, 1)

            def route_second(n, i):
                f = ff[:, n % 2]
                dve.wait_ge(e2_ready, at_loop(n + 1, i, 2))
                link(nc.vector.tensor_scalar(f[:, 7:8], f[:, 6:7], 1.0, None, ALU.add))
                link(nc.vector.reciprocal(f[:, 32:33], f[:, 7:8]))
                link(nc.vector.tensor_tensor(f[:, 33:34], f[:, 32:33], f[:, 6:7], ALU.mult))
                link(nc.vector.tensor_scalar(f[:, 40:48], iota[:], f[:, 24:25], f[:, 32:33], ALU.is_equal, ALU.mult))
                link(nc.vector.tensor_scalar(f[:, 48:56], iota[:], f[:, 25:26], f[:, 33:34], ALU.is_equal, ALU.mult))
                link(nc.vector.tensor_tensor(f[:, 56:64], f[:, 40:48], f[:, 48:56], ALU.add))
                if n >= 2:
                    dve.wait_ge(hw_turned, at_loop(n - 1, i, 2))
                nc.vector.tensor_tensor(hw[:, n % 2].rearrange("p (e r) -> p e r", e=E),
                                        psum[:, 4, 0:E * R].rearrange("p (e r) -> p e r", e=E),
                                        f[:, 56:64, None].broadcast_to((P, E, R)), ALU.mult).then_inc(hw_ready, 1)

            def finish(n, i):
                dve.wait_ge(z_full, at_loop(n + 1, i, 2))
                dve.wait_ge(x1b_ready, at_loop(n + 1, i, 2))
                if n >= 2:
                    dve.wait_ge(out_sem[n % 2], at_loop(16 * (n // 2), i, 16))
                nc.vector.tensor_tensor(y_sb[:, n % 2], x1b[:, n % 2], psum[:, 6 + n % 2], ALU.add).then_inc(y_ready, 1)

            def ffn_step(n, i=None):
                if n < NT:
                    residual(n, i)
                if 1 <= n <= NT:
                    route_first(n - 1, i)
                if n < NT:
                    norm2(n, i)
                if 1 <= n <= NT:
                    route_second(n - 1, i)
                if 2 <= n:
                    finish(n - 2, i)

            dve.wait_ge(x2_in[0], 16)
            ffn_step(0)
            ffn_step(1)
            reciprocals(1)
            ffn_step(2)
            ffn_step(3)
            for c in range(1, NCH):
                dve.wait_ge(x2_in[c], 16)
                with dve.Fori(0, QT // 2) as i:
                    chain.enter(i, 2 * LINKS_PER_TILE)
                    for s in range(2):
                        ffn_step(QT * c + s, i)
                    chain.leave(QT // 2)
            ffn_step(NT)
            ffn_step(NT + 1)

        @block.gpsimd
        def _(pool):
            def store_queries(c, m):
                n = 4 * c + m
                pool.wait_ge(q_split, n + 1)
                if n:
                    pool.wait_ge(q_stored, 16 * n)
                pool.dma_start(q_dram[c, :, P * m:P * (m + 1)].rearrange("a r q -> r a q"),
                               qpart[:, n % 4]).then_inc(q_stored, 16)

            def plain_next():
                pool.nop(nofuse=True)

            def split_max(u, i):
                pool.wait_ge(slot_free, at_loop(NSL * (u // 2) + TURN[u % 2] + 1, i, 2 * NSL))
                if u >= 2:
                    pool.wait_ge(m_stored, at_loop(16 * (u - 1), i, 64))
                plain_next()
                k = 4 * u
                mt, mp = m_t[:, u % 2], m_part[:, u % 2]
                nc.gpsimd.tensor_copy(mp[:, 0], mt).then_inc(pool_chain, 1)
                pool.wait_ge(pool_chain, at_loop(k + 1, i, 16))
                nc.gpsimd.tensor_tensor(out=m_rest[:], in0=mt, in1=mp[:, 0], op=ALU.subtract).then_inc(pool_chain, 1)
                pool.wait_ge(pool_chain, at_loop(k + 2, i, 16))
                plain_next()
                nc.gpsimd.tensor_copy(mp[:, 1], m_rest[:]).then_inc(pool_chain, 1)
                pool.wait_ge(pool_chain, at_loop(k + 3, i, 16))
                nc.gpsimd.tensor_tensor(out=m_rest[:], in0=m_rest[:], in1=mp[:, 1], op=ALU.subtract).then_inc(pool_chain, 1)
                pool.wait_ge(pool_chain, at_loop(k + 4, i, 16))
                plain_next()
                nc.gpsimd.tensor_copy(mp[:, 2], m_rest[:]).then_inc(m_split, 1)

            def zero_future(m, late, i):
                for n, (l, t, off) in enumerate(TILES):
                    if l != late or t < QT * late:
                        continue
                    pool.wait_ge(exp_done, at_loop(NSC * m + SC0[n + 1], i, 2 * NSC))
                    plain_next()
                    d = probs[:, n % 4, :, 0:P]
                    nc.gpsimd.affine_select(out=d, in_=d, compare_op=ALU.is_ge, fill=0.0, base=0,
                                            pattern=[[0, UH], [1, P]], channel_multiplier=-1).then_inc(diag_done, 1)

            def step(k, i=None):
                for late in range(2):
                    if k:
                        zero_future(k - 1, late, i)
                    if k < NK:
                        split_max(2 * k + late, i)
                    if k == NK - 1 and not late:
                        pool.wait_ge(heads_in[0], 16 * 4 * UH)
                        normalise(0, None)
                        normalise(1, None)

            def normalise(n, i):
                c = n // QT
                if n >= 2:
                    pool.wait_ge(y_full, at_loop(n - 1, i, 2))
                tok = bass.ds(at_loop((n % QT) * P, i, 2 * P), P)
                nc.gpsimd.tensor_tensor(out=att[:, n % 2], in0=heads_of(c)[:, :, tok], in1=rcps_of(c)[:, :, tok],
                                        op=ALU.mult).then_inc(att_ready, 1)

            def add_bias(n, i):
                pool.wait_ge(x1_ready, at_loop(n + 1, i, 2))
                if n >= 2:
                    pool.wait_ge(y_ready, at_loop(n - 1, i, 2))
                nc.gpsimd.tensor_tensor(out=x1b[:, n % 2], in0=x1[:, n % 2], in1=bias_sb[:], op=ALU.add).then_inc(x1b_ready, 1)

            def ffn_step(n, i=None):
                if 2 <= n < NT:
                    normalise(n, i)
                if n:
                    add_bias(n - 1, i)

            among = early_slots()
            for c in range(NCH):
                for m in range(4):
                    store_queries(c, m)
                    if TURN[0] in among.get((c, m), ()):
                        split_max(0, None)
            split_max(1, None)
            for b in range(B):
                if b:
                    step(NB * b)
                step(NB * b + 1)
                with pool.Fori(0, PAIRS - 1 - b) as i:
                    step(NB * b + 2, i)
                    step(NB * b + 3, i)
            step(NK - 2)
            step(NK - 1)
            step(NK)

            pool.wait_ge(w2_in, 16 * N_W2)
            for n in range(QT):
                ffn_step(n)
            for c in range(1, NCH):
                pool.wait_ge(heads_in[c], 16 * 4 * UH)
                with pool.Fori(0, QT // 2) as i:
                    for s in range(2):
                        ffn_step(QT * c + s, i)
            ffn_step(NT)


def constants():
    import numpy as np

    bf16 = np.dtype("bfloat16")

    def parts(a, n):
        out, rest = [], np.asarray(a, np.float64)
        for _ in range(n):
            out.append(rest.astype(np.float32).astype(bf16))
            rest = rest - out[-1].astype(np.float64)
        return out

    slopes = ((2.0 ** (-(2.0 ** (3 - np.log2(H))))) ** np.arange(1, H + 1)).astype(np.float32).astype(np.float64)
    pos = np.arange(S, dtype=np.float64)
    slope_rows = [np.broadcast_to(a[:, None], (H, S)) for a in parts(slopes, 3)]
    q_rows = np.stack(slope_rows + slope_rows + parts(-slopes[:, None] * pos[None, :], 4))
    q_rows = q_rows.reshape(N_ALIBI, PAIRS, UH, 2, 2, CH).transpose(0, 4, 1, 3, 2, 5).reshape(N_ALIBI, 2 * H * CH)
    one = np.ones(S)
    stairs = [DH * r for r in range(1, N_STAIR + 1)]
    k_rows = np.stack([pos % P] * 3 + [pos - pos % P] * 3 + [one] * 7 + [pos % P >= r for r in stairs]).astype(bf16)
    kmask = np.zeros((P, 3), np.float32)
    for n, (_, b) in enumerate(PARTS):
        kmask[DH * n:DH * (n + 1), b] = 1.0
    return {
        "ident": np.eye(P, dtype=np.float32),
        "future": np.triu(np.full((P, CH), -1e30, np.float32), CH - P + 1) + 0.0,
        "kmask": kmask,
        "kalibi": k_rows,
        "qalibi": q_rows,
        "stair": np.tile([np.where(pos[:P] < r, -1e30, 0.0) for r in stairs], (1, H * QT)).astype(bf16),
        "iota": np.broadcast_to(np.arange(E, dtype=np.float32), (P, E)).copy(),
    }


def kernel(L0_attn_hidden_states, L0_attn_Wqkv, L0_attn_Wo, L0_ffn_W_base, L0_ffn_b_base, L0_ffn_W_gate, L0_ffn_A, L0_ffn_B):
    import numpy as np
    import concourse.bacc as bacc
    from concourse.bass_utils import run_bass_kernel_spmd as run

    w = np.asarray(L0_attn_Wqkv)
    w_q = w[:, :D].reshape(D, PAIRS, UH, 2, DH).swapaxes(2, 3).reshape(D, D)
    arrays = {
        "x": np.asarray(L0_attn_hidden_states).reshape(B * S, D),
        "wqkv": np.concatenate([w_q] + [w[:, D:D + DH]] * len(PARTS) + [w[:, D + DH:]], axis=1),
        "wo": np.asarray(L0_attn_Wo),
        "wb": np.asarray(L0_ffn_W_base).T,
        "ag": np.concatenate([np.asarray(L0_ffn_A).reshape(E * R, D).T, np.asarray(L0_ffn_W_gate).T], axis=1),
        "lora": np.asarray(L0_ffn_B).transpose(0, 2, 1).reshape(E * R, D),
        "bias": np.broadcast_to(np.asarray(L0_ffn_b_base), (P, D)),
        **constants(),
    }
    nc = bacc.Bacc("TRN2", target_bir_lowering=False, num_devices=1)
    args, fed = [], {}
    for name, a in arrays.items():
        a = np.ascontiguousarray(a)
        fed[f"in_{name}"] = a
        args.append(nc.dram_tensor(f"in_{name}", a.shape, mybir.dt.from_np(a.dtype), kind="ExternalInput").ap())
    out = nc.dram_tensor("out", (B * S, D), F32, kind="ExternalOutput").ap()
    build(nc, *args, out)
    r = run(nc, [fed], core_ids=[0])
    return r.results[0]["out"].reshape(B, S, D)
```
